# Optimizing a Trainium2 kernel written in Bass

```python
import numpy as np
import jax
import jax.numpy as jnp

def _softmax(x, axis=-1):
    return jax.nn.softmax(x, axis=axis)

def _gelu(x):
    return jax.nn.gelu(x, approximate=True)

def _silu(x):
    return jax.nn.silu(x)

def _sigmoid(x):
    return jax.nn.sigmoid(x)

def _layernorm(x, axis=-1, eps=1e-05):
    m = jnp.mean(x, axis=axis, keepdims=True)
    v = jnp.var(x, axis=axis, keepdims=True)
    return (x - m) / jnp.sqrt(v + eps)

def _scatter_add(tgt, idx, src, axis=0):
    return tgt.at[idx].add(src)

def _segment_sum(src, seg, n):
    return jax.ops.segment_sum(src, seg, n)
kernel_name = 'mk_seq_preln_d2_jaxref_r4_504046'

def setup_inputs(seed: int=0):
    np.random.seed(seed)
    _w = jnp.asarray

    def _L0_attn_setup():
        import jax, jax.numpy as jnp
        import numpy as np
        HIDDEN, KEY_DIM, VALUE_DIM = (256, 64, 64)
        B, T = (4, 1024)
        key = jax.random.key(seed)
        ks = jax.random.split(key, 9)
        s = 0.02
        return {'y_all': jax.random.normal(ks[0], (B, T, HIDDEN), dtype=jnp.float32), 'Wq': jax.random.normal(ks[1], (KEY_DIM, HIDDEN), dtype=jnp.float32) * s, 'bq': jax.random.normal(ks[2], (KEY_DIM,), dtype=jnp.float32) * s, 'Wk': jax.random.normal(ks[3], (KEY_DIM, HIDDEN), dtype=jnp.float32) * s, 'bk': jax.random.normal(ks[4], (KEY_DIM,), dtype=jnp.float32) * s, 'Wv': jax.random.normal(ks[5], (VALUE_DIM, HIDDEN), dtype=jnp.float32) * s, 'bv': jax.random.normal(ks[6], (VALUE_DIM,), dtype=jnp.float32) * s, 'Wo': jax.random.normal(ks[7], (HIDDEN, VALUE_DIM), dtype=jnp.float32) * s, 'bo': jax.random.normal(ks[8], (HIDDEN,), dtype=jnp.float32) * s}
    _L0_attn_in = _L0_attn_setup()

    def _L0_ffn_setup():
        import jax, jax.numpy as jnp
        import numpy as np
        FP8_MAX = 448.0
        SCALE = 1.0
        _FP8_DTYPE = getattr(jnp, 'float8_e4m3fn', jnp.float16)

        def quantize_e4m3(t, scale):
            return jnp.clip(t / scale, -FP8_MAX, FP8_MAX).astype(_FP8_DTYPE)
        key = jax.random.key(seed)
        kx, kw = jax.random.split(key)
        B, N, C, F = (8, 1024, 256, 256)
        x = jax.random.normal(kx, (B, N, C), dtype=jnp.float32)
        weight = jax.random.normal(kw, (F, C), dtype=jnp.float32) * 0.02
        bias = jnp.zeros((F,), dtype=jnp.float32)
        return {'x': x, 'weight': weight, 'bias': bias}
    _L0_ffn_in = _L0_ffn_setup()

    def _L1_attn_setup():
        import jax, jax.numpy as jnp
        import numpy as np
        NUM_HEADS = 16
        D_MODEL = 256
        D_K = D_MODEL // NUM_HEADS
        MAX_SEQ_LEN = 1024
        ROPE_BASE = 10000.0
        BATCH = 2
        SEQ_LEN = 512

        def _rope_tables(seq_len, d_k, base=ROPE_BASE):
            theta = 1.0 / base ** (jnp.arange(0, d_k, 2, dtype=jnp.float32) / d_k)
            m = jnp.arange(seq_len, dtype=jnp.float32)
            m_theta = jnp.outer(m, theta)
            ang = jnp.concatenate([m_theta, m_theta], axis=-1)
            return (jnp.cos(ang), jnp.sin(ang))

        def _apply_rope(x, cos, sin):
            d2 = x.shape[-1] // 2
            x1, x2 = (x[..., :d2], x[..., d2:])
            x_flip = jnp.concatenate([-x2, x1], axis=-1)
            return x * cos + x_flip * sin
        key = jax.random.key(seed)
        kx, kq, kk, kv, ko = jax.random.split(key, 5)
        s = 1.0 / np.sqrt(D_MODEL)
        x = jax.random.normal(kx, (BATCH, SEQ_LEN, D_MODEL), dtype=jnp.float32)
        W_Q = jax.random.uniform(kq, (D_MODEL, D_MODEL), jnp.float32, -s, s)
        W_K = jax.random.uniform(kk, (D_MODEL, D_MODEL), jnp.float32, -s, s)
        W_V = jax.random.uniform(kv, (D_MODEL, D_MODEL), jnp.float32, -s, s)
        W_O = jax.random.uniform(ko, (D_MODEL, D_MODEL), jnp.float32, -s, s)
        return {'x': x, 'W_Q': W_Q, 'W_K': W_K, 'W_V': W_V, 'W_O': W_O}
    _L1_attn_in = _L1_attn_setup()

    def _L1_ffn_setup():
        import jax, jax.numpy as jnp
        import numpy as np
        DIM = 256

        def _reference_tuple_inner(x, W_r, W_k, W_v, mu_r, mu_k):
            B, T, C = x.shape
            x_prev = jnp.concatenate([jnp.zeros((B, 1, C), x.dtype), x[:, :-1, :]], axis=1)
            xr = mu_r * x + (1.0 - mu_r) * x_prev
            xk = mu_k * x + (1.0 - mu_k) * x_prev
            r = jax.nn.sigmoid(jnp.einsum('btc,dc->btd', xr, W_r))
            k = jnp.einsum('btc,dc->btd', xk, W_k)
            k_act = jnp.square(jax.nn.relu(k))
            out = r * jnp.einsum('btc,dc->btd', k_act, W_v)
            new_state = x[:, -1, :]
            return (out, new_state)
        key = jax.random.key(seed)
        ks = jax.random.split(key, 6)
        B, T, C = (8, 512, DIM)
        x = jax.random.normal(ks[0], (B, T, C), dtype=jnp.float32)
        s = 1.0 / np.sqrt(C)
        W_r = jax.random.uniform(ks[1], (C, C), jnp.float32, -s, s)
        W_k = jax.random.uniform(ks[2], (C, C), jnp.float32, -s, s)
        W_v = jax.random.uniform(ks[3], (C, C), jnp.float32, -s, s)
        mu_r = jax.random.uniform(ks[4], (C,), jnp.float32)
        mu_k = jax.random.uniform(ks[5], (C,), jnp.float32)
        return {'x': x, 'W_r': W_r, 'W_k': W_k, 'W_v': W_v, 'mu_r': mu_r, 'mu_k': mu_k}
    _L1_ffn_in = _L1_ffn_setup()
    _d = {'L0_attn_y_all': _L0_attn_in['y_all'], 'L0_attn_Wq': _L0_attn_in['Wq'], 'L0_attn_bq': _L0_attn_in['bq'], 'L0_attn_Wk': _L0_attn_in['Wk'], 'L0_attn_bk': _L0_attn_in['bk'], 'L0_attn_Wv': _L0_attn_in['Wv'], 'L0_attn_bv': _L0_attn_in['bv'], 'L0_attn_Wo': _L0_attn_in['Wo'], 'L0_attn_bo': _L0_attn_in['bo'], 'L0_ffn_weight': _L0_ffn_in['weight'], 'L0_ffn_bias': _L0_ffn_in['bias'], 'L1_attn_W_Q': _L1_attn_in['W_Q'], 'L1_attn_W_K': _L1_attn_in['W_K'], 'L1_attn_W_V': _L1_attn_in['W_V'], 'L1_attn_W_O': _L1_attn_in['W_O'], 'L1_ffn_W_r': _L1_ffn_in['W_r'], 'L1_ffn_W_k': _L1_ffn_in['W_k'], 'L1_ffn_W_v': _L1_ffn_in['W_v'], 'L1_ffn_mu_r': _L1_ffn_in['mu_r'], 'L1_ffn_mu_k': _L1_ffn_in['mu_k']}
    _x0 = _d['L0_attn_y_all']
    _d['L0_attn_y_all'] = jax.random.normal(jax.random.fold_in(jax.random.key(seed), 1), (4, 2048, 256), dtype=_x0.dtype)
    del _x0
    return _d

def reference(L0_attn_y_all, L0_attn_Wq, L0_attn_bq, L0_attn_Wk, L0_attn_bk, L0_attn_Wv, L0_attn_bv, L0_attn_Wo, L0_attn_bo, L0_ffn_weight, L0_ffn_bias, L1_attn_W_Q, L1_attn_W_K, L1_attn_W_V, L1_attn_W_O, L1_ffn_W_r, L1_ffn_W_k, L1_ffn_W_v, L1_ffn_mu_r, L1_ffn_mu_k):

    def _L0_attn_ref(y_all, Wq, bq, Wk, bk, Wv, bv, Wo, bo):
        import jax, jax.numpy as jnp
        import numpy as np
        HIDDEN, KEY_DIM, VALUE_DIM = (256, 64, 64)
        B, T = (4, 1024)
        q = jnp.einsum('bth,kh->btk', y_all, Wq) + bq
        k = jnp.einsum('bth,kh->btk', y_all, Wk) + bk
        v = jnp.einsum('bth,vh->btv', y_all, Wv) + bv
        scale = jnp.asarray(KEY_DIM, q.dtype) ** 0.5
        scores = jnp.einsum('bqk,btk->bqt', q / scale, k)
        t = scores.shape[-1]
        causal = jnp.tril(jnp.ones((t, t), dtype=bool))
        scores = jnp.where(causal, scores, jnp.asarray(-jnp.inf, scores.dtype))
        weights = jax.nn.softmax(scores, axis=-1)
        ctx = jnp.einsum('bqt,btv->bqv', weights, v)
        out = jnp.einsum('bqv,hv->bqh', ctx, Wo) + bo
        return out

    def _L0_ffn_ref(x, weight, bias):
        import jax, jax.numpy as jnp
        import numpy as np
        FP8_MAX = 448.0
        SCALE = 1.0
        _FP8_DTYPE = getattr(jnp, 'float8_e4m3fn', jnp.float16)

        def quantize_e4m3(t, scale):
            return jnp.clip(t / scale, -FP8_MAX, FP8_MAX).astype(_FP8_DTYPE)
        B, N, C = x.shape
        x2d = x.reshape(B * N, C)
        x_mat = quantize_e4m3(x2d, SCALE).astype(jnp.float16)
        w_mat = quantize_e4m3(weight, SCALE).astype(jnp.float16)
        out2d = (x_mat @ w_mat.T).astype(jnp.float32) * (SCALE * SCALE)
        out2d = out2d + bias
        return out2d.reshape(B, N, -1)

    def _L1_attn_ref(x, W_Q, W_K, W_V, W_O):
        import jax, jax.numpy as jnp
        import numpy as np
        NUM_HEADS = 16
        D_MODEL = 256
        D_K = D_MODEL // NUM_HEADS
        MAX_SEQ_LEN = 1024
        ROPE_BASE = 10000.0
        BATCH = 2
        SEQ_LEN = 512

        def _rope_tables(seq_len, d_k, base=ROPE_BASE):
            theta = 1.0 / base ** (jnp.arange(0, d_k, 2, dtype=jnp.float32) / d_k)
            m = jnp.arange(seq_len, dtype=jnp.float32)
            m_theta = jnp.outer(m, theta)
            ang = jnp.concatenate([m_theta, m_theta], axis=-1)
            return (jnp.cos(ang), jnp.sin(ang))

        def _apply_rope(x, cos, sin):
            d2 = x.shape[-1] // 2
            x1, x2 = (x[..., :d2], x[..., d2:])
            x_flip = jnp.concatenate([-x2, x1], axis=-1)
            return x * cos + x_flip * sin
        B, S, _ = x.shape

        def proj(W):
            y = jnp.einsum('bsd,ed->bse', x, W)
            return y.reshape(B, S, NUM_HEADS, D_K).transpose(0, 2, 1, 3)
        Q, K, V = (proj(W_Q), proj(W_K), proj(W_V))
        cos, sin = _rope_tables(S, D_K)
        Q = _apply_rope(Q, cos, sin)
        K = _apply_rope(K, cos, sin)
        scores = jnp.einsum('bhsd,bhtd->bhst', Q, K) / jnp.sqrt(jnp.float32(D_K))
        causal = jnp.tril(jnp.ones((S, S), dtype=bool))
        scores = jnp.where(causal[None, None], scores, -jnp.inf)
        attn = jax.nn.softmax(scores, axis=-1)
        out = jnp.einsum('bhst,bhtd->bhsd', attn, V)
        out = out.transpose(0, 2, 1, 3).reshape(B, S, D_MODEL)
        return jnp.einsum('bsd,ed->bse', out, W_O)

    def _L1_ffn_ref(x, W_r, W_k, W_v, mu_r, mu_k):
        import jax, jax.numpy as jnp
        import numpy as np
        DIM = 256

        def _reference_tuple_inner(x, W_r, W_k, W_v, mu_r, mu_k):
            B, T, C = x.shape
            x_prev = jnp.concatenate([jnp.zeros((B, 1, C), x.dtype), x[:, :-1, :]], axis=1)
            xr = mu_r * x + (1.0 - mu_r) * x_prev
            xk = mu_k * x + (1.0 - mu_k) * x_prev
            r = jax.nn.sigmoid(jnp.einsum('btc,dc->btd', xr, W_r))
            k = jnp.einsum('btc,dc->btd', xk, W_k)
            k_act = jnp.square(jax.nn.relu(k))
            out = r * jnp.einsum('btc,dc->btd', k_act, W_v)
            new_state = x[:, -1, :]
            return (out, new_state)
        return _reference_tuple_inner(x, W_r, W_k, W_v, mu_r, mu_k)[0]
    x = L0_attn_y_all
    x = x + _L0_attn_ref(_layernorm(x, axis=-1), L0_attn_Wq, L0_attn_bq, L0_attn_Wk, L0_attn_bk, L0_attn_Wv, L0_attn_bv, L0_attn_Wo, L0_attn_bo)
    x = x + _L0_ffn_ref(_layernorm(x, axis=-1), L0_ffn_weight, L0_ffn_bias)
    x = x + _L1_attn_ref(_layernorm(x, axis=-1), L1_attn_W_Q, L1_attn_W_K, L1_attn_W_V, L1_attn_W_O)
    x = x + _L1_ffn_ref(_layernorm(x, axis=-1), L1_ffn_W_r, L1_ffn_W_k, L1_ffn_W_v, L1_ffn_mu_r, L1_ffn_mu_k)
    return x

_drawn_inputs = setup_inputs


def setup_inputs(seed=0):
    import zlib

    import numpy as np

    out = dict(_drawn_inputs(seed))
    spreads = {'L0_ffn_bias': (0.0, 0.1)}
    factors = {'L0_attn_Wq': 8.0,
     'L0_attn_bq': 8.0,
     'L0_attn_Wk': 8.0,
     'L0_attn_bk': 8.0,
     'L0_attn_Wv': 8.0,
     'L0_attn_bv': 8.0,
     'L0_attn_Wo': 8.0,
     'L0_attn_bo': 2.733,
     'L1_attn_W_Q': 7.556,
     'L1_attn_W_K': 7.262,
     'L1_ffn_W_r': 3.327,
     'L1_ffn_mu_r': 6.77}
    for name, (base, spread) in spreads.items():
        noise = np.random.default_rng([zlib.crc32(name.encode()), seed]).standard_normal(out[name].shape)
        drawn = base * np.exp(spread * noise) if base else spread * noise
        out[name] = jnp.asarray(drawn.astype(out[name].dtype))
    for name, factor in factors.items():
        out[name] = (out[name] * factor).astype(out[name].dtype)
    return out
```

```python
from contextlib import ExitStack

import numpy as np

import concourse.bass as bass
from concourse import mybir

ALU = mybir.AluOpType
ACT = mybir.ActivationFunctionType
AX = mybir.AxisListType
F32 = mybir.dt.float32
F16 = mybir.dt.float16
BF16 = mybir.dt.bfloat16
FP8 = mybir.dt.float8e4

P = 128
B, T, D = 4, 2048, 256
NT = T // P
CH = 512
NQ = T // CH
TPC = CH // P
DC = D // P
EPS = 1e-5
NEG = -1e38

DK0 = 64
H, DK1 = 16, 16
HG = 4
NHG = H // HG
VW = DK1 + 1
PARTS = 3
TERMS = [(0, 0), (0, 1), (0, 2), (1, 0), (1, 1), (2, 0)]
KS = len(TERMS) * DK1
MAXROWS = 2

STAGES = [("T0", 8), ("QK0", 8), ("V0", 2), ("CT0", 4), ("WO0", 8), ("T1", 8), ("FFN", 8), ("T2", 8),
          ("QKR", 32), ("V1", 8), ("AT1", 8), ("WO1", 8), ("T3", 8), ("R", 8), ("K", 8), ("V", 8)]
FIRST = {}
_n = 0
for _name, _count in STAGES:
    FIRST[_name] = _n
    _n += _count
JOBS = _n
EJOBS = JOBS // 2

QKR = [("QK", 0), ("QK", 1), ("RT", 0), ("QK", 2), ("RT", 1), ("QK", 3), ("RT", 2), ("RT", 3)]
QKR_AT = {key: FIRST["QKR"] + TPC * n for n, key in enumerate(QKR)}

UNITS0 = sum(TPC * (q + 1) + 1 for q in range(NQ))
UNITS1 = sum(TPC * (q + 1) for q in range(NQ)) * HG + 1
STEPS = sum(TPC * (q + 1) for q in range(NQ))
SUBS = 2 * STEPS
P1_DELAY = 16


def max_units0():
    units = []
    for q in range(NQ):
        units += [(i, c) for i in range(TPC * q, TPC * (q + 1)) for c in range(q + 1)] + [(None, q)]
    return units


def max_units1():
    return [(i, c, h) for i in range(NT) for c in range(i // TPC + 1) for h in range(HG)] + [None]


def steps():
    return [(q, kb) for q in range(NQ) for kb in range(TPC * (q + 1))]


def span(q, kb):
    return max(0, kb - TPC * q) * P


MAX0, MAX1, ORDER = max_units0(), max_units1(), steps()
assert len(MAX0) == UNITS0 and len(MAX1) == UNITS1 and len(ORDER) == STEPS


def last_block(k):
    q, kb = ORDER[k]
    return kb == TPC * (q + 1) - 1


def plan0():
    plan, unit = [], 0
    for k in range(STEPS + 2):
        if k < STEPS:
            q, kb = ORDER[k]
            if kb == 0:
                for ahead in range(0 if q == 0 else q + 1, min(q + 2, NQ)):
                    while MAX0[unit] != (None, ahead):
                        plan.append(("max", unit))
                        unit += 1
                    plan.append(("max", unit))
                    unit += 1
            plan.append(("scores", k))
        if k >= 2:
            plan.append(("values", k - 2))
            q, kb = ORDER[k - 2]
            if last_block(k - 2):
                plan.append(("copy out", q))
            if q > 0 and kb == 2:
                plan.append(("turn", q - 1))
    plan.append(("turn", NQ - 1))
    return plan


def plan1(g):
    plan = []
    units = UNITS1 if g + 1 < NHG else 0
    done = 0
    for s in range(SUBS + 2):
        if s < SUBS:
            plan.append(("scores", s))
        if s >= 2:
            plan.append(("values", s - 2))
            k, pair = divmod(s - 2, 2)
            q, kb = ORDER[k]
            if pair == 1 and last_block(k):
                plan.append(("copy out", q))
            if pair == 1 and q > 0 and kb == 1:
                plan.append(("turn", q - 1))
        due = units if s >= SUBS - 1 else max(0, (s + 1 - P1_DELAY) * units // (SUBS - P1_DELAY))
        while done < due:
            plan.append(("max", done))
            done += 1
    plan.append(("turn", NQ - 1))
    return plan


def build(nc, x_in, y_out, w):
    ctx = ExitStack()
    with ctx:
        def sb(name, shape, dt):
            return ctx.enter_context(nc.sbuf_tensor(name, shape, dt))

        def sem(name):
            return ctx.enter_context(nc.semaphore(name))

        psum = ctx.enter_context(nc.psum_tensor("psum", [P, 8 * CH], F32))

        def bank(n, lo=0, hi=CH, rows=P, row=0):
            return psum[row:row + rows, n * CH + lo:n * CH + hi]

        x = sb("x", [P, NT, D], F32)
        xn = sb("xn", [P, NT, D], F32)
        xnT = sb("xnT", [P, DC, 1 + T], F32)
        xqT = sb("xqT", [P, DC, T], FP8)
        stats = sb("stats", [P, NT, 6], F32)
        mv = sb("mv", [P, NT, 2], F32)
        vare = sb("vare", [P, NT], F32)
        rstd = sb("rstd", [P, NT], F32)
        mhalf = sb("mhalf", [P, NT], F32)
        ident = sb("ident", [P, P], F32)
        identb = sb("identb", [P, P], BF16)
        maskq = sb("maskq", [P, CH], BF16)
        maskk = sb("maskk", [P, P], BF16)
        cos = sb("cos", [P, NT, DK1], F32)
        sin = sb("sin", [P, NT, DK1], F32)
        wqk0 = sb("wqk0", [P, DC, 2 * DK0], F32)
        wv0 = sb("wv0", [P, DC, DK0], F32)
        wo0 = sb("wo0", [DK0 + 1, D], F32)
        bqk0 = sb("bqk0", [DK0, 2], F32)
        bv0 = sb("bv0", [P, DK0], F32)
        wf = sb("wf", [P, DC, D], BF16)
        wf8 = sb("wf8", [P, 2, DC * D], FP8)
        bf = sb("bf", [P, D], F32)
        wqk1 = sb("wqk1", [P, DC, 2 * D], F32)
        wv1 = sb("wv1", [P, DC, D], F32)
        wo1 = sb("wo1", [P, DC, D], F32)
        wr = sb("wr", [P, DC, D], F32)
        wk = sb("wk", [P, DC, D], F32)
        wv = sb("wv", [P, DC, D], F32)
        mu = sb("mu", [P, 2, DC], F32)
        omu = sb("omu", [P, 2, DC], F32)
        tmp = sb("tmp", [P, 4, 2 * D], F32)
        tmp16 = sb("tmp16", [P, 4, 2 * D], F16)
        stack = sb("stack", [P, 2, 2, HG * T], BF16)
        v1 = sb("v1", [P, NT, H, VW], F32)
        probs = sb("probs", [P, 2 * HG, CH], F32)
        mx0 = sb("mx0", [P, NT, NQ], F32)
        nmax0 = sb("nmax0", [P, NT], F32)
        nmaxT0 = sb("nmaxT0", [TPC, P], F32)
        mx1 = sb("mx1", [P, HG, NT, NQ], F32)
        nmax1 = sb("nmax1", [P, HG * NT], F32)
        nmaxb = sb("nmaxb", [P, MAXROWS, HG * NT], BF16)
        nmaxT1 = sb("nmaxT1", [HG * NT, MAXROWS, P], BF16)
        junk = sb("junk", [P, 4, CH], BF16)
        osb = sb("osb", [P, 2, CH], F32)
        rec = sb("rec", [P, TPC, HG], F32)

        def words(i, side):
            return stack[:, i, side, :].bitcast(F32)

        def tiles(ap, width):
            return ap.rearrange("p (t v) -> p t v", v=width)

        qa = words(0, 0)[0:DK0 + 2, 0:T]
        ka = words(0, 0)[0:DK0 + 2, T:2 * T]
        ctxT = words(0, 1)[0:DK0 + 1, 0:T]
        v0 = tiles(words(1, 0)[:, 0:NT * (DK0 + 1)], DK0 + 1)
        ctx0 = tiles(words(1, 0)[:, T:T + NT * (DK0 + 1)], DK0 + 1)
        xr = words(0, 0).rearrange("p (c t) -> p c t", c=DC)
        xk = words(0, 1).rearrange("p (c t) -> p c t", c=DC)
        gate = tiles(words(1, 0), D)
        kact = words(1, 1).rearrange("p (c t) -> p c t", c=DC)
        qs = [stack[:, i, 0, :].rearrange("p (h t) -> p h t", h=HG) for i in range(2)]
        ks = [stack[:, i, 1, :].rearrange("p (h t) -> p h t", h=HG) for i in range(2)]
        att = xn
        xnf = xn[:, :, :].rearrange("p t d -> p (t d)")
        qcos, qsin, qkc, resid = [[xnf[:, (2 * k + i) * CH:(2 * k + i + 1) * CH] for i in range(2)] for k in range(4)]
        roped = probs
        v1f = v1[:, :, :, :].rearrange("p t h v -> p (t h v)")
        parts = v1f[:, 0:4 * PARTS * CH // 2].bitcast(BF16).rearrange("p (i r n) -> p i r n", i=4, r=PARTS)
        parts_dram = nc.dram_tensor("parts_dram", [2, PARTS, D, T], BF16, kind="Internal").ap()

        s_w0 = sem("s_w0")
        s_w1 = sem("s_w1")
        s_const = sem("s_const")
        s_wq = sem("s_wq")
        s_ready = sem("s_ready")
        s_x = [sem(f"s_x{g}") for g in range(NQ)]
        s_agg = sem("s_agg")
        s_eps = sem("s_eps")
        s_rstd = sem("s_rstd")
        s_norm = sem("s_norm")
        s_mm = sem("s_mm")
        s_ea = sem("s_ea")
        s_ed = sem("s_ed")
        s_fill = sem("s_fill")
        s_xp = sem("s_xp")
        s_xd = sem("s_xd")
        s_p1 = sem("s_p1")
        s_m1 = sem("s_m1")
        s_nm0 = sem("s_nm0")
        s_row0 = sem("s_row0")
        s_s0 = sem("s_s0")
        s_e0 = sem("s_e0")
        s_v0 = sem("s_v0")
        s_oe = sem("s_oe")
        s_ot = sem("s_ot")
        s_oc = sem("s_oc")
        s_rt = sem("s_rt")
        s_rope = sem("s_rope")
        s_re = sem("s_re")
        s_mid = sem("s_mid")
        s_lo = sem("s_lo")
        s_pd = [sem(f"s_pd{i}") for i in range(4)]
        s_stk = [sem(f"s_stk{i}") for i in range(2)]
        s_p2 = sem("s_p2")
        s_m2 = sem("s_m2")
        s_nm1 = sem("s_nm1")
        s_row1 = sem("s_row1")
        s_s1 = sem("s_s1")
        s_e1 = sem("s_e1")
        s_v1 = sem("s_v1")
        s_mix = sem("s_mix")
        s_gate = sem("s_gate")
        s_ku = sem("s_ku")
        s_out = sem("s_out")
        s_link = sem("s_link")
        s_pl = sem("s_pl")
        s_apart = sem("s_apart")

        XJOBS = 4 * 4
        PJOBS = 4 * NQ
        OUTS = NQ + NHG * NQ
        STK = 16 * 2 * len(TERMS)
        FILLS = 7
        LINKS = 4 * NQ + 2 * NQ + 2 * NHG + NHG * NQ + 4 + NQ
        PLINKS = 4 + 4
        NCONST = 9
        W0, W1 = 16 * 10, 16 * 7

        def apart(eng):
            eng.sem_inc(s_apart, 1)

        def parts_out(eng, b):
            for i in range(4):
                eng.wait_ge(s_pd[i], b * 4 * PJOBS + 4 * PJOBS)

        block = ctx.enter_context(nc.Block())

        @block.sync
        def _(sp):
            def cw(a):
                return a.rearrange("(c p) n -> p c n", p=P)

            for dst, src in [
                (wqk0[:, :, :], cw(w["wqk0"])),
                (wv0[:, :, :], cw(w["wv0"])),
                (wo0[0:DK0, :], w["wo0"]),
                (wo0[DK0:DK0 + 1, :], w["bo0"].rearrange("(a d) -> a d", a=1)),
                (bqk0[:, :], w["bqk0"]),
                (bv0[:, :], w["bv0"].rearrange("(a d) -> a d", a=1).broadcast_to([P, DK0])),
                (tmp[:, 0, :].rearrange("p (c d) -> p c d", c=DC), cw(w["wf"])),
                (bf[:, :], w["bf"].rearrange("(a d) -> a d", a=1).broadcast_to([P, D])),
                (cos[:, :, :], w["cos"].rearrange("(t p) d -> p t d", p=P)),
                (sin[:, :, :], w["sin"].rearrange("(t p) d -> p t d", p=P)),
            ]:
                sp.dma_start(dst, src).then_inc(s_w0, 16)

            with sp.Fori(0, B) as b:
                for g in range(NQ):
                    sp.dma_start(x[:, TPC * g:TPC * (g + 1), :],
                                 x_in[bass.ds(b, 1), CH * g:CH * (g + 1), :]
                                 .rearrange("o (t p) d -> p (o t) d", p=P)).then_inc(s_x[g], 16)
                for q in range(NQ):
                    sp.wait_ge(s_m1, b * UNITS0 + MAX0.index((None, q)) + 1)
                    sp.dma_start(qa[DK0 + 1:DK0 + 2, CH * q:CH * (q + 1)], nmaxT0[:, :]).then_inc(s_row0, 16)
                for n in range(PJOBS):
                    g, bl = divmod(n, 4)
                    sp.wait_ge(s_lo, b * PJOBS + n + 1)
                    sp.dma_start(
                        parts_dram[bl // 2, :, (bl % 2) * P:(bl % 2 + 1) * P, CH * g:CH * (g + 1)]
                        .rearrange("r p n -> p r n"), parts[:, n % 4, :, :]).then_inc(s_pd[n % 4], 16)

                def load_stack(hg):
                    for side in range(2):
                        to = (qs, ks)[side][hg % 2]
                        for n, term in enumerate(TERMS):
                            rows = parts_dram[side, term[side], HG * DK1 * hg:HG * DK1 * (hg + 1), :]
                            sp.dma_start(to[DK1 * n:DK1 * (n + 1), :, :],
                                         rows.rearrange("(h d) t -> d h t", h=HG)).then_inc(s_stk[hg % 2], 16)

                parts_out(sp, b)
                load_stack(0)
                load_stack(1)
                for hg in range(NHG):
                    sp.wait_ge(s_m2, b * NHG * UNITS1 + UNITS1 * (hg + 1))
                    for r in range(MAXROWS):
                        sp.dma_start(stack[KS + r:KS + r + 1, hg % 2, 0, :],
                                     nmaxT1[:, r, :]).then_inc(s_row1, 16)
                    if 1 <= hg < NHG - 1:
                        sp.wait_ge(s_s1, b * NHG * SUBS + SUBS * hg)
                        load_stack(hg + 1)
                for g in range(NQ):
                    sp.wait_ge(s_xp, b * XJOBS + XJOBS - NQ + g + 1)
                    apart(sp)
                    sp.wait_ge(s_xd, b * 8 + 4 + g + 1)
                    apart(sp)
                    sp.dma_start(y_out[bass.ds(b, 1), CH * g:CH * (g + 1), :]
                                 .rearrange("o (t p) d -> p (o t) d", p=P),
                                 x[:, TPC * g:TPC * (g + 1), :]).then_inc(s_out, 16)
                sp.wait_ge(s_out, b * 16 * NQ + 16 * NQ)
                apart(sp)

        @block.gpsimd
        def _(pool):
            pool.memset(ident[:, :], 0.0).then_inc(s_const, 1)
            pool.memset(maskq[:, :], 0.0).then_inc(s_const, 1)
            pool.memset(maskk[:, :], 0.0).then_inc(s_const, 1)
            pool.memset(mhalf[:, :], -0.5).then_inc(s_const, 1)
            pool.memset(xnT[:, :, 0:1], 0.0).then_inc(s_const, 1)
            pool.wait_ge(s_const, 5)
            pool.affine_select(out=ident[:, :], in_=ident[:, :], compare_op=ALU.not_equal, fill=1.0,
                               base=0, pattern=[[-1, P]], channel_multiplier=1).then_inc(s_const, 1)
            pool.affine_select(out=maskq[:, CH - P:CH], in_=maskq[:, CH - P:CH], compare_op=ALU.is_ge, fill=NEG,
                               base=0, pattern=[[-1, P]], channel_multiplier=1).then_inc(s_const, 1)
            pool.affine_select(out=maskk[:, :], in_=maskk[:, :], compare_op=ALU.is_ge, fill=NEG,
                               base=0, pattern=[[1, P]], channel_multiplier=-1).then_inc(s_const, 1)
            pool.wait_ge(s_const, 8)
            pool.tensor_copy(identb[:, :], ident[:, :]).then_inc(s_const, 1)

            with pool.Fori(0, B) as b:
                plinks = [0]

                def plink(ins):
                    plinks[0] += 1
                    ins.then_inc(s_pl, 1)
                    pool.wait_ge(s_pl, b * PLINKS + plinks[0])

                def roots(ln):
                    for g in range(NQ):
                        ts = slice(TPC * g, TPC * (g + 1))
                        pool.wait_ge(s_agg, b * 4 * NQ + ln * NQ + g + 1)
                        apart(pool)
                        pool.tensor_scalar(vare[:, ts], mv[:, ts, 1], EPS, None, ALU.add).then_inc(s_eps, 1)
                        pool.wait_ge(s_eps, b * 4 * NQ + ln * NQ + g + 1)
                        pool.tensor_tensor(rstd[:, ts], vare[:, ts], mhalf[:, ts], ALU.pow).then_inc(s_rstd, 1)

                def read_by_act(stage, e):
                    pool.wait_ge(s_ea, b * EJOBS + FIRST[stage] // 2 + e + 1)

                def add_jobs(stage):
                    for e in range(4):
                        xs = x[:, 4 * e:4 * e + 2, :].rearrange("p t d -> p (t d)")
                        read_by_act(stage, e)
                        pool.tensor_tensor(xs, xs, tmp[:, e % 2, :], ALU.add).then_inc(s_xp, 1)

                roots(0)
                pool.wait_ge(s_rstd, b * 4 * NQ + NQ)
                fills = [(qa[DK0:DK0 + 2, :], 0.0), (ka[DK0:DK0 + 2, :], 1.0),
                         (v0[:, :, DK0:DK0 + 1], 1.0), (ctx0[:, :, DK0:DK0 + 1], 1.0),
                         (stack[KS:P, 0, 1, :], 1.0), (stack[KS:P, 1, 1, :], 1.0)]
                for n, (rows, value) in enumerate(fills):
                    if n > 0:
                        pool.wait_ge(s_fill, b * FILLS + n)
                    apart(pool)
                    pool.memset(rows, value).then_inc(s_fill, 1)
                pool.wait_ge(s_fill, b * FILLS + len(fills))
                add_jobs("WO0")
                roots(1)
                for e in range(4):
                    xs = x[:, 4 * e:4 * e + 2, :]
                    t2 = tmp[:, e % 2, :].rearrange("p (t d) -> p t d", t=2)
                    read_by_act("FFN", e)
                    plink(pool.tensor_tensor(t2, tmp16[:, e % 2, :].rearrange("p (t d) -> p t d", t=2),
                                             bf[:, :].unsqueeze(1).broadcast_to([P, 2, D]), ALU.add))
                    pool.tensor_tensor(xs, xs, t2, ALU.add).then_inc(s_xp, 1)
                roots(2)
                for k, (key, g) in enumerate(QKR):
                    for i in range(TPC):
                        if key == "QK":
                            t = TPC * g + i
                            if i % 2 == 0:
                                pool.wait_ge(s_rt, b * (NT // 2) + t // 2 + 1)
                            else:
                                pool.wait_ge(s_ed, b * EJOBS + (FIRST["QKR"] + TPC * k + i) // 2 + 1)
                            pool.tensor_tensor(roped[:, t % 8, :], qcos[t % 2], qsin[t % 2],
                                               ALU.add).then_inc(s_rope, 1)
                        else:
                            n = 4 * g + i
                            pool.wait_ge(s_re, b * PJOBS + n + 1)
                            apart(pool)
                            pool.tensor_copy(parts[:, n % 4, 1, :], resid[n % 2]).then_inc(s_mid, 1)
                            pool.wait_ge(s_mid, b * PJOBS + n + 1)
                            pool.tensor_tensor(parts[:, n % 4, 2, :], resid[n % 2], parts[:, n % 4, 1, :],
                                               ALU.subtract).then_inc(s_lo, 1)
                parts_out(pool, b)
                apart(pool)
                pool.memset(v1[:, :, :, DK1:VW], 1.0).then_inc(s_fill, 1)
                add_jobs("WO1")
                roots(3)
                for n in range(8):
                    q, c = divmod(n, DC)
                    if n % 2 == 0:
                        read_by_act("K", n // 2)
                    else:
                        pool.wait_ge(s_ed, b * EJOBS + FIRST["K"] // 2 + n // 2 + 1)
                    u = tmp[:, (n % 2) * 2 + n // 2 % 2, :]
                    pool.tensor_tensor(kact[:, c, CH * q:CH * (q + 1)], u, u, ALU.mult).then_inc(s_ku, 1)
                for e in range(4):
                    xs = x[:, 4 * e:4 * e + 2, :].rearrange("p t d -> p (t d)")
                    gs = gate[:, 4 * e:4 * e + 2, :].rearrange("p t d -> p (t d)")
                    read_by_act("V", e)
                    plink(pool.tensor_tensor(tmp[:, e % 2, :], tmp[:, e % 2, :], gs, ALU.mult))
                    pool.tensor_tensor(xs, xs, tmp[:, e % 2, :], ALU.add).then_inc(s_xp, 1)
                assert plinks[0] == PLINKS

        @block.scalar
        def _(act):
            def cw(a):
                return a.rearrange("(c p) n -> p c n", p=P)

            for dst, src in [
                (wqk1[:, :, :], cw(w["wqk1"])), (wv1[:, :, :], cw(w["wv1"])), (wo1[:, :, :], cw(w["wo1"])),
                (wr[:, :, :], cw(w["wr"])), (wk[:, :, :], cw(w["wk"])), (wv[:, :, :], cw(w["wv"])),
                (mu[:, :, :], w["mu"]),
            ]:
                act.dma_start(dst, src).then_inc(s_w1, 16)
            act.wait_ge(s_w0, W0)

            with act.Fori(0, B) as b:
                def job(stage, e):
                    j = FIRST[stage] + 2 * e
                    act.wait_ge(s_mm, b * JOBS + j + 1)
                    return bank(j // 2 % 4)

                def turned(stage, dst=xnT, col=1):
                    for g in range(NQ):
                        ps = job(stage, g)
                        apart(act)
                        if dst is xqT:
                            ins = act.activation(dst[:, 0, CH * g:CH * (g + 1)], ps, ACT.Copy, saturate=False)
                        else:
                            ins = act.activation(dst[:, 0, 1 + CH * g:1 + CH * (g + 1)], ps, ACT.Copy)
                        ins.then_inc(s_ea, 1)

                def to_pool(stage, dst, func, used, per_batch, count):
                    for e in range(4):
                        ps = job(stage, e)
                        if e >= 2:
                            act.wait_ge(used, b * per_batch + count(e - 2))
                        elif stage == "V":
                            act.wait_ge(s_ku, b * 8 + 2 * e + 5)
                        act.activation(dst[:, e % 2, :], ps, func).then_inc(s_ea, 1)

                turned("T0")
                for q in range(NQ):
                    ps = job("QK0", q)
                    act.activation(qa[0:DK0, CH * q:CH * (q + 1)], ps[0:DK0, :], ACT.Identity,
                                   bias=bqk0[:, 0:1]).then_inc(s_ea, 1)
                ps = job("V0", 0)
                act.activation(v0[:, 0:NT // 2, 0:DK0], tiles(ps, DK0), ACT.Copy).then_inc(s_ea, 1)
                for k, (q, kb) in enumerate(ORDER):
                    off = span(q, kb)
                    if k >= 4:
                        act.wait_ge(s_v0, b * STEPS + k - 3)
                    act.wait_ge(s_s0, b * STEPS + k + 1)
                    act.activation(probs[:, k % 4, 0:CH - off], bank(k % 4, 0, CH - off), ACT.Exp,
                                   scale=DK0 ** -0.5).then_inc(s_e0, 1)
                for e in range(2):
                    ps = job("CT0", e)
                    act.activation(ctxT[:, 2 * CH * e:2 * CH * e + CH], ps[0:DK0 + 1, :],
                                   ACT.Copy).then_inc(s_ea, 1)
                to_pool("WO0", tmp, ACT.Copy, s_xp, XJOBS, lambda e: e + 1)
                turned("T1", xqT)
                to_pool("FFN", tmp16, ACT.Copy, s_xp, XJOBS, lambda e: 4 + e + 1)
                turned("T2")
                for n, (key, g) in enumerate(QKR):
                    for i in range(0, TPC, 2):
                        ps = job("QKR", (TPC * n + i) // 2)
                        if key == "QK":
                            t = TPC * g + i
                            if t >= 4:
                                act.wait_ge(s_rt, b * (NT // 2) + t // 2 - 1)
                            act.activation(qkc[t // 2 % 2], ps, ACT.Copy).then_inc(s_ea, 1)
                        else:
                            m = 4 * g + i
                            if m >= 2:
                                act.wait_ge(s_lo, b * PJOBS + m - 1)
                            if m >= 4:
                                act.wait_ge(s_pd[m % 4], b * 4 * PJOBS + 16 * (m // 4))
                            act.activation(resid[m % 2], ps, ACT.Copy)
                            act.activation(parts[:, m % 4, 0, :], ps, ACT.Copy).then_inc(s_ea, 1)
                parts_out(act, b)
                for e in range(4):
                    ps = job("V1", e)
                    act.activation(v1[:, 4 * e:4 * e + 2, :, 0:DK1],
                                   ps.rearrange("p (t h v) -> p t h v", t=2, h=H), ACT.Copy).then_inc(s_ea, 1)
                for hg in range(NHG):
                    for s in range(SUBS):
                        k, pair = divmod(s, 2)
                        off = span(*ORDER[k])
                        at = SUBS * hg + s
                        if at >= 4:
                            act.wait_ge(s_v1, b * NHG * SUBS + at - 3)
                        act.wait_ge(s_s1, b * NHG * SUBS + at + 1)
                        two = psum[:, 2 * pair * CH:2 * (pair + 1) * CH].rearrange("p (h n) -> p h n", h=2)
                        at = HG * (k % 2) + 2 * pair
                        act.activation(probs[:, at:at + 2, 0:CH - off], two[:, :, 0:CH - off], ACT.Exp,
                                       scale=DK1 ** -0.5).then_inc(s_e1, 1)
                turned("AT1")
                to_pool("WO1", tmp, ACT.Copy, s_xp, XJOBS, lambda e: 8 + e + 1)
                turned("T3")
                for e in range(4):
                    ps = job("R", e)
                    act.activation(gate[:, 4 * e:4 * e + 2, :], tiles(ps, D), ACT.Sigmoid).then_inc(s_ea, 1)
                    act.wait_ge(s_ed, b * EJOBS + FIRST["R"] // 2 + e + 1)
                    act.activation(gate[:, 4 * e + 2:4 * e + 4, :], gate[:, 4 * e + 2:4 * e + 4, :],
                                   ACT.Sigmoid).then_inc(s_gate, 1)
                to_pool("K", tmp, ACT.Relu, s_ku, 8, lambda e: 2 * e + 1)
                to_pool("V", tmp, ACT.Copy, s_xp, XJOBS, lambda e: 12 + e + 1)

        @block.vector
        def _(dve):
            chain = [0]

            def then(ins):
                chain[0] += 1
                ins.then_inc(s_wq, 1)
                dve.wait_ge(s_wq, chain[0])

            raw, small, large, pick = (tmp[:, i, :] for i in range(4))
            dve.wait_ge(s_w0, W0)
            dve.tensor_tensor(pick, raw, raw, ALU.mult)
            dve.tensor_scalar(small, raw, 128.0, -128.0, ALU.min, ALU.max)
            then(dve.tensor_scalar(large, raw, 448.0, -448.0, ALU.min, ALU.max))
            dve.tensor_scalar(pick, pick, 128.0 ** 2, None, ALU.is_gt)
            dve.tensor_copy(wf8[:, 0, :], small, saturate=False)
            then(dve.tensor_scalar(wf8[:, 1, :], large, 0.5, None, ALU.mult, saturate=False))
            dve.tensor_copy(small, wf8[:, 0, :])
            then(dve.tensor_scalar(large, wf8[:, 1, :], 2.0, None, ALU.mult))
            then(dve.tensor_tensor(large, large, small, ALU.subtract))
            then(dve.tensor_tensor(large, large, pick, ALU.mult))
            dve.tensor_tensor(wf[:, :, :].rearrange("p c d -> p (c d)"), small, large, ALU.add)
            dve.memset(mx1[:, :, :, :], -3e38)
            dve.memset(psum[:, :], 0.0)
            dve.wait_ge(s_w1, W1)
            dve.tensor_scalar(omu[:, :, :], mu[:, :, :], -1.0, 1.0, ALU.mult, ALU.add).then_inc(s_ready, 1)
            dve.wait_ge(s_const, NCONST)

            with dve.Fori(0, B) as b:
                links = [0]

                def link(ins):
                    links[0] += 1
                    ins.then_inc(s_link, 1)
                    dve.wait_ge(s_link, b * LINKS + links[0])

                def norm(ln):
                    def statistics(g):
                        if ln == 0:
                            dve.wait_ge(s_x[g], b * 16 + 16)
                        else:
                            dve.wait_ge(s_xp, b * XJOBS + 4 * (ln - 1) + g + 1)
                            if ln == 2:
                                dve.wait_ge(s_xd, b * 8 + g + 1)
                            else:
                                stage = {1: "WO0", 3: "WO1"}[ln]
                                dve.wait_ge(s_ed, b * EJOBS + FIRST[stage] // 2 + g + 1)
                        for t in range(TPC * g, TPC * (g + 1)):
                            last = dve.bn_stats(stats[:, t, :], x[:, t, :])
                        link(last)
                        apart(dve)
                        for t in range(TPC * g, TPC * (g + 1)):
                            last = dve.bn_aggr(mv[:, t, :], stats[:, t, :])
                        last.then_inc(s_agg, 1)

                    def scale(g):
                        dve.wait_ge(s_rstd, b * 4 * NQ + ln * NQ + g + 1)
                        for t in range(TPC * g, TPC * (g + 1)):
                            last = dve.tensor_scalar(xn[:, t, :], x[:, t, :], mv[:, t, 0:1], rstd[:, t:t + 1],
                                                     ALU.subtract, ALU.mult)
                        last.then_inc(s_norm, 1)

                    statistics(0)
                    for g in range(1, NQ):
                        statistics(g)
                        scale(g - 1)
                    scale(NQ - 1)

                def job(stage, e):
                    j = FIRST[stage] + 2 * e + 1
                    dve.wait_ge(s_mm, b * JOBS + j + 1)
                    return bank(4 + j // 2 % 4)

                def turned(stage, dst=xnT):
                    for g in range(NQ):
                        ps = job(stage, g)
                        apart(dve)
                        col = 0 if dst is xqT else 1
                        kind = {"saturate": False} if dst is xqT else {}
                        dve.tensor_copy(dst[:, 1, col + CH * g:col + CH * (g + 1)], ps, **kind).then_inc(s_ed, 1)

                def add_jobs(stage):
                    for e in range(4):
                        ps = job(stage, e)
                        xs = x[:, 4 * e + 2:4 * e + 4, :]
                        dve.tensor_tensor(xs, tiles(ps, D), xs, ALU.add).then_inc(s_ed, 1)

                norm(0)
                turned("T0")
                for q in range(NQ):
                    ps = job("QK0", q)
                    dve.tensor_scalar(ka[0:DK0, CH * q:CH * (q + 1)], ps[0:DK0, :], bqk0[:, 1:2], None,
                                      ALU.add).then_inc(s_ed, 1)
                ps = job("V0", 0)
                dve.tensor_copy(v0[:, NT // 2:NT, 0:DK0], tiles(ps, DK0)).then_inc(s_ed, 1)

                def read_scores(ps, n, diagonal, out, slot):
                    if diagonal:
                        apart(dve)
                        ins = dve.tensor_tensor_reduce(junk[:, slot, 0:n], ps, maskq[:, CH - n:CH], 1.0, -3e38,
                                                       ALU.add, ALU.max, out)
                    else:
                        ins = dve.tensor_reduce(out, ps, AX.X, ALU.max)
                    return ins

                def copy_out(oq, rows):
                    dve.tensor_copy(osb[0:rows, oq % 2, :], bank(6 + oq % 2, rows=rows)).then_inc(s_oe, 1)

                for kind, n in plan0():
                    if kind == "max":
                        i, c = MAX0[n]
                        ps = bank(4 + n % 2)
                        if i is None:
                            dve.wait_ge(s_m1, b * UNITS0 + n)
                            ts = slice(TPC * c, TPC * (c + 1))
                            dve.tensor_reduce(nmax0[:, ts], mx0[:, ts, 0:c + 1], AX.X, ALU.max,
                                              negate=True).then_inc(s_nm0, 1)
                            dve.wait_ge(s_p1, b * UNITS0 + n + 1)
                            if c >= 1:
                                dve.wait_ge(s_row0, b * 16 * NQ + 16 * c)
                            dve.tensor_copy(nmaxT0[:, :], ps[0:TPC, 0:P]).then_inc(s_m1, 1)
                        else:
                            width = CH if c < i // TPC else (i % TPC + 1) * P
                            if n >= 4:
                                dve.wait_ge(s_m1, b * UNITS0 + n - 3)
                            dve.wait_ge(s_p1, b * UNITS0 + n + 1)
                            read_scores(ps[:, 0:width], width, c == i // TPC, mx0[:, i, c:c + 1],
                                        n % 4).then_inc(s_m1, 1)
                    elif kind == "copy out":
                        dve.wait_ge(s_v0, b * STEPS + ORDER.index((n, TPC * (n + 1) - 1)) + 1)
                        copy_out(n, DK0 + 1)
                    elif kind == "turn":
                        dve.wait_ge(s_ot, b * OUTS + n + 1)
                        turned_o = tiles(bank(6 + n % 2), P)
                        ts = slice(TPC * n, TPC * (n + 1))
                        link(dve.reciprocal(rec[:, :, 0], turned_o[:, :, DK0]))
                        link(dve.tensor_tensor(ctx0[:, ts, 0:DK0], turned_o[:, :, 0:DK0],
                                               rec[:, :, 0:1].broadcast_to([P, TPC, DK0]), ALU.mult))
                        dve.tensor_tensor(ctx0[:, ts, 0:DK0], ctx0[:, ts, 0:DK0],
                                          bv0[:, :].unsqueeze(1).broadcast_to([P, TPC, DK0]),
                                          ALU.add).then_inc(s_oc, 1)
                for e in range(2):
                    ps = job("CT0", e)
                    dve.tensor_copy(ctxT[:, CH * (2 * e + 1):CH * (2 * e + 2)], ps[0:DK0 + 1, :]).then_inc(s_ed, 1)
                add_jobs("WO0")
                norm(1)
                turned("T1", xqT)
                for e in range(4):
                    ps = job("FFN", e)
                    xs = x[:, 4 * e + 2:4 * e + 4, :]
                    t16, t32 = tiles(tmp16[:, 2 + e % 2, :], D), tiles(tmp[:, 2 + e % 2, :], D)
                    dve.tensor_copy(t16, tiles(ps, D)).then_inc(s_ed, 1)
                    dve.wait_ge(s_ed, b * EJOBS + FIRST["FFN"] // 2 + e + 1)
                    link(dve.tensor_tensor(t32, t16, bf[:, :].unsqueeze(1).broadcast_to([P, 2, D]), ALU.add))
                    dve.tensor_tensor(xs, xs, t32, ALU.add).then_inc(s_xd, 1)
                norm(2)
                turned("T2")
                for n, (key, g) in enumerate(QKR):
                    for i in range(TPC):
                        if key == "QK":
                            t = TPC * g + i
                            if i % 2 == 0:
                                dve.wait_ge(s_ea, b * EJOBS + (FIRST["QKR"] + TPC * n + i) // 2 + 1)
                                src = qkc[t // 2 % 2]
                            else:
                                src = job("QKR", (TPC * n + i) // 2)
                            if t >= 2:
                                dve.wait_ge(s_rope, b * NT + t - 1)
                            src = src.rearrange("p (h d) -> p h d", d=DK1)
                            half = DK1 // 2
                            to_cos = qcos[t % 2].rearrange("p (h d) -> p h d", d=DK1)
                            to_sin = qsin[t % 2].rearrange("p (h d) -> p h d", d=DK1)
                            cs = cos[:, t, :].unsqueeze(1)
                            sn = sin[:, t, :].unsqueeze(1)
                            dve.tensor_tensor(to_cos, src, cs.broadcast_to([P, 2 * H, DK1]), ALU.mult)
                            dve.tensor_tensor(to_sin[:, :, 0:half], src[:, :, half:DK1],
                                              sn[:, :, 0:half].broadcast_to([P, 2 * H, half]), ALU.mult)
                            ins = dve.tensor_tensor(to_sin[:, :, half:DK1], src[:, :, 0:half],
                                                    sn[:, :, half:DK1].broadcast_to([P, 2 * H, half]), ALU.mult)
                            ins.then_inc(s_ed if i % 2 else s_rt, 1)
                        else:
                            m = 4 * g + i
                            if i % 2 == 1:
                                ps = job("QKR", (TPC * n + i) // 2)
                                if m >= 2:
                                    dve.wait_ge(s_lo, b * PJOBS + m - 1)
                                if m >= 4:
                                    dve.wait_ge(s_pd[m % 4], b * 4 * PJOBS + 16 * (m // 4))
                                dve.tensor_copy(resid[m % 2], ps)
                                dve.tensor_copy(parts[:, m % 4, 0, :], ps).then_inc(s_ed, 1)
                            dve.wait_ge(s_ed if i % 2 else s_ea,
                                        b * EJOBS + (FIRST["QKR"] + TPC * n + i) // 2 + 1)
                            dve.tensor_tensor(resid[m % 2], resid[m % 2], parts[:, m % 4, 0, :],
                                              ALU.subtract).then_inc(s_re, 1)
                parts_out(dve, b)
                for e in range(4):
                    ps = job("V1", e)
                    dve.tensor_copy(v1[:, 4 * e + 2:4 * e + 4, :, 0:DK1].rearrange("p t h v -> p (t h) v"),
                                    tiles(ps, DK1)).then_inc(s_ed, 1)

                def attention1(hg, plan):
                    for kind, n in plan:
                        if kind == "max":
                            at = UNITS1 * (hg + 1) + n
                            ps = bank(4 + at % 2)
                            if MAX1[n] is None:
                                dve.wait_ge(s_m2, b * NHG * UNITS1 + at)
                                if hg >= 0:
                                    dve.wait_ge(s_row1, b * 16 * MAXROWS * NHG + 16 * MAXROWS * (hg + 1))
                                link(dve.tensor_reduce(nmax1[:, :], mx1[:, :, :, :].rearrange("p h t c -> p (h t) c"),
                                                       AX.X, ALU.max, negate=True))
                                link(dve.tensor_copy(nmaxb[:, 0, :], nmax1[:, :]))
                                dve.tensor_tensor(nmaxb[:, 1, :], nmax1[:, :], nmaxb[:, 0, :],
                                                  ALU.subtract).then_inc(s_nm1, 1)
                                dve.wait_ge(s_p2, b * NHG * UNITS1 + at + 1)
                                dve.tensor_copy(nmaxT1[:, :, :],
                                                ps.bitcast(BF16)[0:HG * NT, 0:MAXROWS * P]
                                                .rearrange("p (r n) -> p r n", r=MAXROWS)).then_inc(s_m2, 1)
                            else:
                                i, c, h = MAX1[n]
                                width = CH if c < i // TPC else (i % TPC + 1) * P
                                if at >= 4:
                                    dve.wait_ge(s_m2, b * NHG * UNITS1 + at - 3)
                                dve.wait_ge(s_p2, b * NHG * UNITS1 + at + 1)
                                read_scores(ps[:, 0:width], width, c == i // TPC,
                                            mx1[:, h, i, c:c + 1], at % 4).then_inc(s_m2, 1)
                        elif kind == "copy out":
                            oq = NQ * (hg + 1) + n
                            k = ORDER.index((n, TPC * (n + 1) - 1))
                            dve.wait_ge(s_v1, b * NHG * SUBS + SUBS * hg + 2 * k + 2)
                            copy_out(oq, P)
                        elif kind == "turn":
                            oq = NQ * (hg + 1) + n
                            dve.wait_ge(s_ot, b * OUTS + oq + 1)
                            turned_o = bank(6 + oq % 2).rearrange("p (t h v) -> p t h v", t=TPC, h=HG)
                            link(dve.reciprocal(rec[:, :, :], turned_o[:, :, :, DK1]))
                            ts = slice(TPC * n, TPC * (n + 1))
                            cols = att[:, ts, HG * DK1 * hg:HG * DK1 * (hg + 1)]
                            dve.tensor_tensor(cols.rearrange("p t (h v) -> p t h v", h=HG),
                                              turned_o[:, :, :, 0:DK1],
                                              rec[:, :, :].unsqueeze(3).broadcast_to([P, TPC, HG, DK1]),
                                              ALU.mult).then_inc(s_oc, 1)

                attention1(-1, [("max", n) for n in range(UNITS1)])
                for hg in range(NHG):
                    attention1(hg, plan1(hg))
                turned("AT1")
                add_jobs("WO1")
                norm(3)
                turned("T3")
                for g in range(NQ):
                    dve.wait_ge(s_ea, b * EJOBS + FIRST["T3"] // 2 + g + 1)
                    dve.wait_ge(s_ed, b * EJOBS + FIRST["T3"] // 2 + g + 1)
                    ts = slice(CH * g, CH * (g + 1))
                    pairs = [(to, i, c) for i, to in enumerate((xr, xk)) for c in range(DC)]
                    for to, i, c in pairs:
                        last = dve.tensor_scalar(to[:, c, ts], xnT[:, c, ts], omu[:, i, c:c + 1], None, ALU.mult)
                    link(last)
                    for to, i, c in pairs:
                        last = dve.scalar_tensor_tensor(out=to[:, c, ts], in0=xnT[:, c, 1 + CH * g:1 + CH * (g + 1)],
                                                        scalar=mu[:, i, c:c + 1], in1=to[:, c, ts],
                                                        op0=ALU.mult, op1=ALU.add)
                    last.then_inc(s_mix, 1)
                for e in range(4):
                    ps = job("R", e)
                    dve.tensor_copy(gate[:, 4 * e + 2:4 * e + 4, :], tiles(ps, D)).then_inc(s_ed, 1)
                for e in range(4):
                    ps = job("K", e)
                    if e >= 2:
                        dve.wait_ge(s_ku, b * 8 + 2 * e - 2)
                    dve.tensor_scalar(tmp[:, 2 + e % 2, :], ps, 0.0, None, ALU.max).then_inc(s_ed, 1)
                for e in range(4):
                    ps = job("V", e)
                    dve.wait_ge(s_gate, b * 4 + e + 1)
                    if e < 2:
                        dve.wait_ge(s_ku, b * 8 + 2 * e + 6)
                    xs = x[:, 4 * e + 2:4 * e + 4, :]
                    t32 = tiles(tmp[:, 2 + e % 2, :], D)
                    dve.tensor_tensor(t32, tiles(ps, D), gate[:, 4 * e + 2:4 * e + 4, :], ALU.mult).then_inc(s_ed, 1)
                    dve.wait_ge(s_ed, b * EJOBS + FIRST["V"] // 2 + e + 1)
                    dve.tensor_tensor(xs, xs, t32, ALU.add).then_inc(s_xd, 1)
                assert links[0] == LINKS, (links[0], LINKS)

        @block.tensor
        def _(pe):
            pe.wait_ge(s_w0, W0)
            pe.wait_ge(s_const, NCONST)
            pe.wait_ge(s_ready, 1)

            with pe.Fori(0, B) as b:
                def job(stage, n):
                    j = FIRST[stage] + n
                    e = j // 2
                    if e >= 4:
                        pe.wait_ge(s_ed if j % 2 else s_ea, b * EJOBS + e - 3)
                    return bank((4 if j % 2 else 0) + e % 4)

                def jobs_read(stage):
                    pe.wait_ge(s_ea, b * EJOBS + FIRST[stage] // 2)
                    pe.wait_ge(s_ed, b * EJOBS + FIRST[stage] // 2)

                def turn(stage, src, ready):
                    for g in range(NQ):
                        ready(g)
                        for c in range(DC):
                            ps = job(stage, 2 * g + c)
                            for i in range(TPC):
                                last = pe.transpose(ps[:, i * P:(i + 1) * P],
                                                    src[:, TPC * g + i, c * P:(c + 1) * P], ident[:, :])
                            last.then_inc(s_mm, 1)

                def normalised(ln):
                    return lambda g: pe.wait_ge(s_norm, b * 4 * NQ + ln * NQ + g + 1)

                def turned(stage, g):
                    pe.wait_ge(s_ea, b * EJOBS + FIRST[stage] // 2 + g + 1)
                    pe.wait_ge(s_ed, b * EJOBS + FIRST[stage] // 2 + g + 1)

                def by_tiles(stage, lhs, rhs, ready, chunks=DC):
                    for n in range(NT // 2):
                        if n % 2 == 0:
                            ready(n // 2)
                        ps = job(stage, n)
                        if stage == "FFN":
                            apart(pe)
                        for i in range(2):
                            for c in range(chunks):
                                last = pe.matmul(ps[:, i * D:(i + 1) * D], lhs(c, 2 * n + i), rhs(c),
                                                 start=(c == 0), stop=(c == chunks - 1))
                        last.then_inc(s_mm, 1)

                def tok(c, t):
                    return xnT[:, c, 1 + P * t:1 + P * (t + 1)]

                turn("T0", xn, normalised(0))
                for n in range(2 * NQ):
                    q, side = divmod(n, 2)
                    if side == 0:
                        turned("T0", q)
                    ps = job("QK0", n)
                    for c in range(DC):
                        last = pe.matmul(ps[0:DK0, :], wqk0[:, c, side * DK0:(side + 1) * DK0],
                                         xnT[:, c, 1 + CH * q:1 + CH * (q + 1)], start=(c == 0), stop=(c == DC - 1))
                    last.then_inc(s_mm, 1)
                for n in range(2):
                    ps = job("V0", n)
                    for i in range(NT // 2):
                        for c in range(DC):
                            last = pe.matmul(ps[:, i * DK0:(i + 1) * DK0], tok(c, NT // 2 * n + i), wv0[:, c, :],
                                             start=(c == 0), stop=(c == DC - 1))
                    last.then_inc(s_mm, 1)

                jobs_read("CT0")
                pe.wait_ge(s_fill, b * FILLS + 4)
                for kind, n in plan0():
                    if kind == "max":
                        i, c = MAX0[n]
                        if n >= 2:
                            pe.wait_ge(s_m1, b * UNITS0 + n - 1)
                        ps = bank(4 + n % 2)
                        if i is None:
                            pe.wait_ge(s_nm0, b * NQ + c + 1)
                            pe.transpose(ps[0:TPC, 0:P], nmax0[:, TPC * c:TPC * (c + 1)], ident[:, :]).then_inc(s_p1, 1)
                        else:
                            width = CH if c < i // TPC else (i % TPC + 1) * P
                            pe.matmul(ps[:, 0:width], qa[0:DK0 + 1, P * i:P * (i + 1)],
                                      ka[0:DK0 + 1, CH * c:CH * c + width], start=True, stop=True).then_inc(s_p1, 1)
                    elif kind == "scores":
                        q, kb = ORDER[n]
                        off = span(q, kb)
                        if kb == 0:
                            pe.wait_ge(s_row0, b * 16 * NQ + 16 * (q + 1))
                        if n >= 4:
                            pe.wait_ge(s_e0, b * STEPS + n - 3)
                        diagonal = kb >= TPC * q
                        ins = pe.matmul(bank(n % 4, 0, CH - off), ka[0:DK0 + 2, P * kb:P * (kb + 1)],
                                        qa[0:DK0 + 2, CH * q + off:CH * (q + 1)], start=True, stop=not diagonal)
                        if diagonal:
                            ins = pe.matmul(bank(n % 4, 0, P), identb[:, :], maskk[:, :], start=False, stop=True)
                        ins.then_inc(s_s0, 1)
                    elif kind == "values":
                        q, kb = ORDER[n]
                        off = span(q, kb)
                        if kb == 0 and q >= 2:
                            pe.wait_ge(s_oc, b * OUTS + q - 1)
                        pe.wait_ge(s_e0, b * STEPS + n + 1)
                        pe.matmul(bank(6 + q % 2, off, CH, rows=DK0 + 1), v0[:, kb, :], probs[:, n % 4, 0:CH - off],
                                  start=(kb == 0), stop=last_block(n)).then_inc(s_v0, 1)
                    elif kind == "turn":
                        pe.wait_ge(s_oe, b * OUTS + n + 1)
                        for i in range(TPC):
                            ins = pe.transpose(bank(6 + n % 2, P * i, P * i + DK0 + 1),
                                               osb[0:DK0 + 1, n % 2, P * i:P * (i + 1)],
                                               ident[0:DK0 + 1, 0:DK0 + 1])
                        ins.then_inc(s_ot, 1)
                pe.wait_ge(s_oc, b * OUTS + NQ)
                for n in range(NQ):
                    ps = job("CT0", n)
                    apart(pe)
                    for i in range(TPC):
                        last = pe.transpose(ps[0:DK0 + 1, P * i:P * (i + 1)], ctx0[:, TPC * n + i, :], ident[:, :])
                    last.then_inc(s_mm, 1)

                def context(g):
                    pe.wait_ge(s_ed if g % 2 else s_ea, b * EJOBS + FIRST["CT0"] // 2 + g // 2 + 1)

                by_tiles("WO0", lambda c, t: ctxT[:, P * t:P * (t + 1)], lambda c: wo0[:, :], context, 1)

                turn("T1", xn, normalised(1))
                by_tiles("FFN", lambda c, t: xqT[:, c, P * t:P * (t + 1)], lambda c: wf[:, c, :],
                         lambda g: turned("T1", g))

                turn("T2", xn, normalised(2))
                for n, (key, g) in enumerate(QKR):
                    if key == "QK":
                        turned("T2", g)
                    else:
                        pe.wait_ge(s_rope, b * NT + TPC * (g + 1))
                    for i in range(TPC):
                        ps = job("QKR", TPC * n + i)
                        if key == "QK":
                            for c in range(DC):
                                last = pe.matmul(ps, tok(c, TPC * g + i), wqk1[:, c, :],
                                                 start=(c == 0), stop=(c == DC - 1))
                        else:
                            for t in range(TPC):
                                last = pe.transpose(ps[:, P * t:P * (t + 1)],
                                                    roped[:, (TPC * g + t) % 8, P * i:P * (i + 1)], ident[:, :])
                        last.then_inc(s_mm, 1)
                by_tiles("V1", tok, lambda c: wv1[:, c, :], lambda g: None)

                def attention1(hg, plan):
                    for kind, n in plan:
                        if kind == "max":
                            at = UNITS1 * (hg + 1) + n
                            if n == 0:
                                pe.wait_ge(s_stk[(hg + 1) % 2], b * STK * NHG // 2 + STK * ((hg + 1) // 2 + 1))
                            if at >= 2:
                                pe.wait_ge(s_m2, b * NHG * UNITS1 + at - 1)
                            ps = bank(4 + at % 2)
                            if MAX1[n] is None:
                                pe.wait_ge(s_nm1, b * NHG + hg + 2)
                                apart(pe)
                                for r in range(MAXROWS):
                                    ins = pe.transpose(ps.bitcast(BF16)[0:HG * NT, P * r:P * (r + 1)],
                                                       nmaxb[:, r, :], identb[:, :])
                                ins.then_inc(s_p2, 1)
                            else:
                                i, c, h = MAX1[n]
                                width = CH if c < i // TPC else (i % TPC + 1) * P
                                side = (hg + 1) % 2
                                pe.matmul(ps[:, 0:width], qs[side][0:KS, h, P * i:P * (i + 1)],
                                          ks[side][0:KS, h, CH * c:CH * c + width],
                                          start=True, stop=True).then_inc(s_p2, 1)
                        elif kind == "scores":
                            k, pair = divmod(n, 2)
                            q, kb = ORDER[k]
                            off = span(q, kb)
                            at = SUBS * hg + n
                            if n == 0:
                                pe.wait_ge(s_row1, b * 16 * MAXROWS * NHG + 16 * MAXROWS * (hg + 1))
                            if at >= 2:
                                pe.wait_ge(s_e1, b * NHG * SUBS + at - 1)
                            diagonal = kb >= TPC * q
                            rows = slice(0, KS + MAXROWS)
                            for h in range(2 * pair, 2 * pair + 2):
                                ins = pe.matmul(bank(h, 0, CH - off), ks[hg % 2][rows, h, P * kb:P * (kb + 1)],
                                                qs[hg % 2][rows, h, CH * q + off:CH * (q + 1)],
                                                start=True, stop=not diagonal)
                                if diagonal:
                                    ins = pe.matmul(bank(h, 0, P), identb[:, :], maskk[:, :], start=False, stop=True)
                            ins.then_inc(s_s1, 1)
                        elif kind == "values":
                            k, pair = divmod(n, 2)
                            q, kb = ORDER[k]
                            off = span(q, kb)
                            oq = NQ * (hg + 1) + q
                            if kb == 0 and pair == 0 and oq >= NQ + 2:
                                pe.wait_ge(s_oc, b * OUTS + oq - 1)
                            pe.wait_ge(s_e1, b * NHG * SUBS + SUBS * hg + n + 1)
                            for h in range(2 * pair, 2 * pair + 2):
                                ins = pe.matmul(bank(6 + oq % 2, off, CH, rows=VW, row=32 * h),
                                                v1[:, kb, HG * hg + h, :], probs[:, HG * (k % 2) + h, 0:CH - off],
                                                start=(kb == 0), stop=last_block(k))
                            ins.then_inc(s_v1, 1)
                        elif kind == "turn":
                            oq = NQ * (hg + 1) + n
                            pe.wait_ge(s_oe, b * OUTS + oq + 1)
                            for i in range(TPC):
                                ins = pe.transpose(bank(6 + oq % 2, P * i, P * (i + 1)),
                                                   osb[:, oq % 2, P * i:P * (i + 1)], ident[:, :])
                            ins.then_inc(s_ot, 1)

                jobs_read("AT1")
                pe.wait_ge(s_fill, b * FILLS + FILLS)
                attention1(-1, [("max", n) for n in range(UNITS1)])
                for hg in range(NHG):
                    attention1(hg, plan1(hg))
                turn("AT1", att, lambda g: pe.wait_ge(s_oc, b * OUTS + OUTS))
                by_tiles("WO1", tok, lambda c: wo1[:, c, :], lambda g: turned("AT1", g))

                turn("T3", xn, normalised(3))
                pe.wait_ge(s_w1, W1)
                by_tiles("R", lambda c, t: xr[:, c, P * t:P * (t + 1)], lambda c: wr[:, c, :],
                         lambda g: pe.wait_ge(s_mix, b * NQ + g + 1))
                for n in range(2 * NQ):
                    q, half = divmod(n, DC)
                    ps = job("K", n)
                    for c in range(DC):
                        last = pe.matmul(ps, wk[:, c, P * half:P * (half + 1)], xk[:, c, CH * q:CH * (q + 1)],
                                         start=(c == 0), stop=(c == DC - 1))
                    last.then_inc(s_mm, 1)
                by_tiles("V", lambda c, t: kact[:, c, P * t:P * (t + 1)], lambda c: wv[:, c, :],
                         lambda g: pe.wait_ge(s_ku, b * 8 + 2 * (g + 1)))


def rope_tables():
    theta = (np.float32(1.0) / np.float32(10000.0) ** (np.arange(0, DK1, 2, dtype=np.float32) / np.float32(DK1)))
    angle = np.outer(np.arange(T, dtype=np.float32), theta.astype(np.float32)).astype(np.float32)
    angle = np.concatenate([angle, angle], axis=-1)
    sign = np.where(np.arange(DK1) < DK1 // 2, np.float32(-1), np.float32(1))
    return np.cos(angle).astype(np.float32), (np.sin(angle) * sign).astype(np.float32)


def arrays(inputs):
    a = {k.replace("L0_attn_", "a0_").replace("L0_ffn_", "f0_").replace("L1_attn_", "a1_").replace("L1_ffn_", "f1_"):
         np.asarray(v) for k, v in inputs.items()}
    c, s = rope_tables()
    w = {
        "wqk0": np.concatenate([a["a0_Wq"], a["a0_Wk"]]).T, "wv0": a["a0_Wv"].T, "wo0": a["a0_Wo"].T,
        "bqk0": np.stack([a["a0_bq"], a["a0_bk"]]).T, "bv0": a["a0_bv"], "bo0": a["a0_bo"],
        "wf": a["f0_weight"].T, "bf": a["f0_bias"],
        "wqk1": np.concatenate([a["a1_W_Q"], a["a1_W_K"]]).T, "wv1": a["a1_W_V"].T, "wo1": a["a1_W_O"].T,
        "wr": a["f1_W_r"].T, "wk": a["f1_W_k"].T, "wv": a["f1_W_v"].T,
        "mu": np.stack([a["f1_mu_r"], a["f1_mu_k"]]).reshape(2, DC, P).transpose(2, 0, 1), "cos": c, "sin": s,
    }
    return a["a0_y_all"], {k: np.ascontiguousarray(v) for k, v in w.items()}


def kernel(**inputs):
    import concourse.bacc as bacc
    from concourse.bass_utils import run_bass_kernel_spmd

    nc = bacc.Bacc("TRN2", target_bir_lowering=False, num_devices=1)
    x, w = arrays(inputs)
    x_in = nc.dram_tensor("x_in", x.shape, F32, kind="ExternalInput").ap()
    aps = {k: nc.dram_tensor("w_" + k, v.shape, F32, kind="ExternalInput").ap() for k, v in w.items()}
    y = nc.dram_tensor("y_out", (B, T, D), F32, kind="ExternalOutput").ap()
    build(nc, x_in, y, aps)
    r = run_bass_kernel_spmd(nc, [{"x_in": x, **{"w_" + k: v for k, v in w.items()}}], core_ids=[0])
    return r.results[0]["y_out"]
```

```python
from contextlib import ExitStack

import numpy as np

import concourse.bass as bass
from concourse import mybir

ALU = mybir.AluOpType
ACT = mybir.ActivationFunctionType
AX = mybir.AxisListType
F32 = mybir.dt.float32
F16 = mybir.dt.float16
BF16 = mybir.dt.bfloat16
FP8 = mybir.dt.float8e4

P = 128
B, T, D = 4, 2048, 256
NT = T // P
CH = 512
NQ = T // CH
TPC = CH // P
DC = D // P
EPS = 1e-5
NEG = -1e38

DK0 = 64
H, DK1 = 16, 16
HG = 4
NHG = H // HG
VW = DK1 + 1
PARTS = 3
TERMS = [(0, 0), (0, 1), (0, 2), (1, 0), (1, 1), (2, 0)]
KS = len(TERMS) * DK1
MAXROWS = 2

STAGES = [("T0", 8), ("QK0", 8), ("V0", 2), ("CT0", 4), ("WO0", 8), ("T1", 8), ("FFN", 8), ("T2", 8),
          ("QKR", 32), ("V1", 8), ("AT1", 8), ("WO1", 8), ("T3", 8), ("R", 8), ("K", 8), ("V", 8)]
FIRST = {}
_n = 0
for _name, _count in STAGES:
    FIRST[_name] = _n
    _n += _count
JOBS = _n
EJOBS = JOBS // 2

QKR = [("QK", 0), ("QK", 1), ("RT", 0), ("QK", 2), ("RT", 1), ("QK", 3), ("RT", 2), ("RT", 3)]
QKR_AT = {key: FIRST["QKR"] + TPC * n for n, key in enumerate(QKR)}

UNITS0 = sum(TPC * (q + 1) + 1 for q in range(NQ))
STEPS = sum(TPC * (q + 1) for q in range(NQ))
SUBS = 2 * STEPS
MB = 3


def max_units0():
    units = []
    for q in range(NQ):
        units += [(i, c) for i in range(TPC * q, TPC * (q + 1)) for c in range(q + 1)] + [(None, q)]
    return units


def steps():
    return [(q, kb) for q in range(NQ) for kb in range(TPC * (q + 1))]


def span(q, kb):
    return max(0, kb - TPC * q) * P


MAX0, ORDER = max_units0(), steps()
assert len(MAX0) == UNITS0 and len(ORDER) == STEPS


def last_block(k):
    q, kb = ORDER[k]
    return kb == TPC * (q + 1) - 1


def plan0():
    plan, unit = [], 0
    for k in range(STEPS + 2):
        if k < STEPS:
            q, kb = ORDER[k]
            if kb == 0:
                for ahead in range(0 if q == 0 else q + 1, min(q + 2, NQ)):
                    while MAX0[unit] != (None, ahead):
                        plan.append(("max", unit))
                        unit += 1
                    plan.append(("max", unit))
                    unit += 1
            plan.append(("scores", k))
        if k >= 2:
            plan.append(("values", k - 2))
            q, kb = ORDER[k - 2]
            if last_block(k - 2):
                plan.append(("copy out", q))
            if q > 0 and kb == 2:
                plan.append(("turn", q - 1))
    plan.append(("turn", NQ - 1))
    return plan


def plan1():
    first, second = [], []
    for g in range(NHG):
        for q in range(NQ):
            block = [("max", (g, i, c, h)) for i in range(TPC * q, TPC * (q + 1))
                     for c in range(q + 1) for h in range(HG)]
            if g + q > 0:
                block.insert(2, ("turned max", divmod(NQ * g + q - 1, NQ)))
            first += block + [("minus max", (g, q))]
    first.append(("turned max", (NHG - 1, NQ - 1)))
    for n in range(NHG * STEPS + 1):
        if n < NHG * STEPS:
            g, k = divmod(n, STEPS)
            second += [("scores", (g, 2 * k)), ("scores", (g, 2 * k + 1))]
        if n > 0:
            second.append(("values", divmod(n - 1, STEPS)))

    hop = 0.1
    plan, read, weights, rows = [], [], [], {}
    loaded = {0: 0.0, 1: 20.0}
    tensor = vector = scalar = copied = 0.0
    n1 = n2 = 0

    def unit_width(item):
        if item[0] != "max":
            return P * TPC
        _, i, c, _ = item[1]
        return CH if c < i // TPC else (i % TPC + 1) * P

    def unit(item):
        nonlocal tensor, vector
        plan.append(item)
        size = unit_width(item) / CH
        free = read[-MB] + hop if len(read) >= MB else 0.0
        tensor = max(tensor, free) + {"turned out": 0.86, "turned max": 0.11}.get(item[0], 0.216 * size)
        vector = max(vector, tensor + hop) + {"turned out": 0.6, "turned max": 0.2}.get(item[0], 0.08 + 0.533 * size)
        read.append(vector)
        if item[0] == "turned max":
            rows[item[1]] = vector + 4.5

    while n2 < len(second):
        unit_at = step_at = 1e9
        if n1 < len(first):
            free = read[-MB] + hop if len(read) >= MB else 0.0
            unit_at = max(tensor, free, loaded.get(first[n1][1][0], 1e9))
        kind, (g, s) = second[n2]
        k = s // 2 if kind == "scores" else s
        q, kb = ORDER[k]
        size = (CH - span(q, kb)) / CH
        if kind == "scores":
            done = weights[-2] + hop if len(weights) >= 2 else 0.0
            step_at = max(tensor, done, rows.get((g, q), 1e9))
        else:
            step_at = max(tensor, weights[2 * (STEPS * g + k) + 1] + hop, copied if kb == 0 else 0.0)
        if unit_at < 1e9 and (unit_at < tensor + 0.05 and vector - tensor < EAGER or unit_at < step_at - 0.05):
            tensor = unit_at
            item = first[n1]
            n1 += 1
            if item[0] == "minus max":
                plan.append(item)
                vector += 0.5
            else:
                unit(item)
            continue
        n2 += 1
        plan.append((kind, (g, s)))
        if kind == "scores":
            tensor = step_at + 0.44 * size + (0.11 if kb >= TPC * q else 0.0)
            scalar = max(scalar, tensor + hop) + 0.05 + 0.853 * size
            weights.append(scalar)
            if s == SUBS - 1:
                loaded[g + 2] = tensor + 18.0
        else:
            tensor = step_at + 0.92 * size
            if last_block(k):
                plan.append(("copy out", (g, q)))
                scalar = max(scalar, tensor + hop) + 0.48
                copied = scalar + hop
            if kb == 2 and (g, q) != (0, 0):
                unit(("turned out", divmod(NQ * g + q - 1, NQ)))
    plan.append(("turned out", (NHG - 1, NQ - 1)))
    assert n1 == len(first)
    return plan


EAGER = 0.9
PLAN1 = plan1()
UNIT1 = {item: n for n, item in enumerate(x for x in PLAN1 if x[0] in ("max", "turned max", "turned out"))}
UNITS1 = len(UNIT1)


def build(nc, x_in, y_out, w):
    ctx = ExitStack()
    with ctx:
        def sb(name, shape, dt):
            return ctx.enter_context(nc.sbuf_tensor(name, shape, dt))

        def sem(name):
            return ctx.enter_context(nc.semaphore(name))

        psum = ctx.enter_context(nc.psum_tensor("psum", [P, 8 * CH], F32))

        def bank(n, lo=0, hi=CH, rows=P, row=0):
            return psum[row:row + rows, n * CH + lo:n * CH + hi]

        x = sb("x", [P, NT, D], F32)
        xn = sb("xn", [P, NT, D], F32)
        xnT = sb("xnT", [P, DC, 1 + T], F32)
        xqT = sb("xqT", [P, DC, T], FP8)
        stats = sb("stats", [P, NT, 6], F32)
        mv = sb("mv", [P, NT, 2], F32)
        vare = sb("vare", [P, NT], F32)
        rstd = sb("rstd", [P, NT], F32)
        mhalf = sb("mhalf", [P, NT], F32)
        ident = sb("ident", [P, P], F32)
        identb = sb("identb", [P, P], BF16)
        maskq = sb("maskq", [P, CH], BF16)
        maskk = sb("maskk", [P, P], BF16)
        cos = sb("cos", [P, NT, DK1], F32)
        sin = sb("sin", [P, NT, DK1], F32)
        wqk0 = sb("wqk0", [P, DC, 2 * DK0], F32)
        wv0 = sb("wv0", [P, DC, DK0], F32)
        wo0 = sb("wo0", [DK0 + 1, D], F32)
        bqk0 = sb("bqk0", [DK0, 2], F32)
        bv0 = sb("bv0", [P, DK0], F32)
        wf = sb("wf", [P, DC, D], BF16)
        wf8 = sb("wf8", [P, 2, DC * D], FP8)
        bf = sb("bf", [P, D], F32)
        wqk1 = sb("wqk1", [P, DC, 2 * D], F32)
        wv1 = sb("wv1", [P, DC, D], F32)
        wo1 = sb("wo1", [P, DC, D], F32)
        wr = sb("wr", [P, DC, D], F32)
        wk = sb("wk", [P, DC, D], F32)
        wv = sb("wv", [P, DC, D], F32)
        mu = sb("mu", [P, 2, DC], F32)
        omu = sb("omu", [P, 2, DC], F32)
        tmp = sb("tmp", [P, 4, 2 * D], F32)
        tmp16 = sb("tmp16", [P, 4, 2 * D], F16)
        stack = sb("stack", [P, 2, 2, HG * T], BF16)
        v1 = sb("v1", [P, NT, H, VW], F32)
        probs = sb("probs", [P, 2 * HG, CH], F32)
        mx0 = sb("mx0", [P, NT, NQ], F32)
        nmax0 = sb("nmax0", [P, NT], F32)
        nmaxT0 = sb("nmaxT0", [TPC, P], F32)
        mx1 = sb("mx1", [P, HG, NT, NQ], F32)
        nmax1 = sb("nmax1", [P, HG * TPC], F32)
        nmaxb = sb("nmaxb", [P, HG, MAXROWS, TPC], BF16)
        nmaxT1 = sb("nmaxT1", [HG * MAXROWS * TPC, 2, P], BF16)
        junk = sb("junk", [P, 4, CH], BF16)
        osb = sb("osb", [P, 2, CH], F32)
        rec = sb("rec", [P, TPC, HG], F32)

        def words(i, side):
            return stack[:, i, side, :].bitcast(F32)

        def tiles(ap, width):
            return ap.rearrange("p (t v) -> p t v", v=width)

        qa = words(0, 0)[0:DK0 + 2, 0:T]
        ka = words(0, 0)[0:DK0 + 2, T:2 * T]
        ctxT = words(0, 1)[0:DK0 + 1, 0:T]
        v0 = tiles(words(1, 0)[:, 0:NT * (DK0 + 1)], DK0 + 1)
        ctx0 = tiles(words(1, 0)[:, T:T + NT * (DK0 + 1)], DK0 + 1)
        xr = words(0, 0).rearrange("p (c t) -> p c t", c=DC)
        xk = words(0, 1).rearrange("p (c t) -> p c t", c=DC)
        gate = tiles(words(1, 0), D)
        kact = words(1, 1).rearrange("p (c t) -> p c t", c=DC)
        qs = [stack[:, i, 0, :].rearrange("p (h t) -> p h t", h=HG) for i in range(2)]
        ks = [stack[:, i, 1, :].rearrange("p (h t) -> p h t", h=HG) for i in range(2)]
        att = xn
        xnf = xn[:, :, :].rearrange("p t d -> p (t d)")
        qcos, qsin, qkc = [[xnf[:, (2 * k + i) * CH:(2 * k + i + 1) * CH] for i in range(2)] for k in range(3)]
        resid = [tmp[:, i, :] for i in range(4)]
        roped = probs
        v1f = v1[:, :, :, :].rearrange("p t h v -> p (t h v)")
        parts = v1f[:, 0:4 * PARTS * CH // 2].bitcast(BF16).rearrange("p (i r n) -> p i r n", i=4, r=PARTS)
        parts_dram = nc.dram_tensor("parts_dram", [2, PARTS, D, T], BF16, kind="Internal").ap()

        s_w0 = sem("s_w0")
        s_w1 = sem("s_w1")
        s_const = sem("s_const")
        s_wq = sem("s_wq")
        s_ready = sem("s_ready")
        s_x = [sem(f"s_x{g}") for g in range(NQ)]
        s_agg = sem("s_agg")
        s_eps = sem("s_eps")
        s_rstd = sem("s_rstd")
        s_norm = sem("s_norm")
        s_mm = sem("s_mm")
        s_ea = sem("s_ea")
        s_ed = sem("s_ed")
        s_fill = sem("s_fill")
        s_xp = sem("s_xp")
        s_xd = sem("s_xd")
        s_p1 = sem("s_p1")
        s_m1 = sem("s_m1")
        s_nm0 = sem("s_nm0")
        s_row0 = sem("s_row0")
        s_s0 = sem("s_s0")
        s_e0 = sem("s_e0")
        s_v0 = sem("s_v0")
        s_oe = sem("s_oe")
        s_ot = sem("s_ot")
        s_oc = sem("s_oc")
        s_rt = sem("s_rt")
        s_rope = sem("s_rope")
        s_re = sem("s_re")
        s_mid = sem("s_mid")
        s_lo = sem("s_lo")
        s_pd = [sem(f"s_pd{i}") for i in range(4)]
        s_first = [sem(f"s_first{q}") for q in range(NQ)]
        s_stk = [sem(f"s_stk{i}") for i in range(2)]
        s_p2 = sem("s_p2")
        s_m2 = sem("s_m2")
        s_nm1 = sem("s_nm1")
        s_row1 = [sem(f"s_row1{i}") for i in range(2)]
        s_o1 = sem("s_o1")
        s_s1 = sem("s_s1")
        s_e1 = sem("s_e1")
        s_v1 = sem("s_v1")
        s_mix = sem("s_mix")
        s_gate = sem("s_gate")
        s_ku = sem("s_ku")
        s_out = sem("s_out")
        s_link = sem("s_link")
        s_pl = sem("s_pl")
        s_apart = sem("s_apart")

        XJOBS = 4 * 4
        PJOBS = 4 * NQ
        OUTS = NHG * NQ
        ROWS = 16 * HG
        STK = 16 * 2 * len(TERMS)
        STKS = [len(range(i, NHG, 2)) - (i == 0) for i in range(2)]
        FILLS = 7
        LINKS = 4 * NQ + 2 * NQ + 2 * OUTS + OUTS + 4 + NQ
        PLINKS = 4 + 4
        NCONST = 9
        W0, W1 = 16 * 10, 16 * 7

        def apart(eng):
            eng.sem_inc(s_apart, 1)

        def parts_out(eng, b):
            for i in range(4):
                eng.wait_ge(s_pd[i], b * 4 * PJOBS + 4 * PJOBS)

        block = ctx.enter_context(nc.Block())

        @block.sync
        def _(sp):
            def cw(a):
                return a.rearrange("(c p) n -> p c n", p=P)

            for dst, src in [
                (wqk0[:, :, :], cw(w["wqk0"])),
                (wv0[:, :, :], cw(w["wv0"])),
                (wo0[0:DK0, :], w["wo0"]),
                (wo0[DK0:DK0 + 1, :], w["bo0"].rearrange("(a d) -> a d", a=1)),
                (bqk0[:, :], w["bqk0"]),
                (bv0[:, :], w["bv0"].rearrange("(a d) -> a d", a=1).broadcast_to([P, DK0])),
                (tmp[:, 0, :].rearrange("p (c d) -> p c d", c=DC), cw(w["wf"])),
                (bf[:, :], w["bf"].rearrange("(a d) -> a d", a=1).broadcast_to([P, D])),
                (cos[:, :, :], w["cos"].rearrange("(t p) d -> p t d", p=P)),
                (sin[:, :, :], w["sin"].rearrange("(t p) d -> p t d", p=P)),
            ]:
                sp.dma_start(dst, src).then_inc(s_w0, 16)

            with sp.Fori(0, B) as b:
                for g in range(NQ):
                    sp.dma_start(x[:, TPC * g:TPC * (g + 1), :],
                                 x_in[bass.ds(b, 1), CH * g:CH * (g + 1), :]
                                 .rearrange("o (t p) d -> p (o t) d", p=P)).then_inc(s_x[g], 16)
                for q in range(NQ):
                    sp.wait_ge(s_m1, b * UNITS0 + MAX0.index((None, q)) + 1)
                    sp.dma_start(qa[DK0 + 1:DK0 + 2, CH * q:CH * (q + 1)], nmaxT0[:, :]).then_inc(s_row0, 16)
                def load_stack(hg, cols, loaded):
                    for side in range(2):
                        to = (qs, ks)[side][hg % 2]
                        for n, term in enumerate(TERMS):
                            rows = parts_dram[side, term[side], HG * DK1 * hg:HG * DK1 * (hg + 1), cols]
                            sp.dma_start(to[DK1 * n:DK1 * (n + 1), :, cols],
                                         rows.rearrange("(h d) t -> d h t", h=HG)).then_inc(loaded, 16)

                for n in range(PJOBS):
                    g, bl = divmod(n, 4)
                    sp.wait_ge(s_lo, b * PJOBS + n + 1)
                    sp.dma_start(
                        parts_dram[bl // 2, :, (bl % 2) * P:(bl % 2 + 1) * P, CH * g:CH * (g + 1)]
                        .rearrange("r p n -> p r n"), parts[:, n % 4, :, :]).then_inc(s_pd[n % 4], 16)

                    if bl == 3:
                        sp.wait_ge(s_pd[0], b * 4 * PJOBS + 16 * (g + 1))
                        apart(sp)
                        sp.wait_ge(s_pd[2], b * 4 * PJOBS + 16 * (g + 1))
                        apart(sp)
                        load_stack(0, slice(CH * g, CH * (g + 1)), s_first[g])
                parts_out(sp, b)
                load_stack(1, slice(0, T), s_stk[1])
                for kind, item in PLAN1:
                    if kind == "turned max":
                        hg, q = item
                        oq = NQ * hg + q
                        sp.wait_ge(s_m2, b * UNITS1 + UNIT1[kind, item] + 1)
                        for h in range(HG):
                            sp.dma_start(qs[hg % 2][KS:KS + MAXROWS, h, CH * q:CH * (q + 1)],
                                         nmaxT1[MAXROWS * TPC * h:MAXROWS * TPC * (h + 1), oq % 2, :]
                                         ).then_inc(s_row1[oq % 2], 16)
                    elif kind == "scores" and item[1] == SUBS - 1 and item[0] + 2 < NHG:
                        sp.wait_ge(s_s1, b * NHG * SUBS + SUBS * (item[0] + 1))
                        load_stack(item[0] + 2, slice(0, T), s_stk[item[0] % 2])
                for g in range(NQ):
                    sp.wait_ge(s_xp, b * XJOBS + XJOBS - NQ + g + 1)
                    apart(sp)
                    sp.wait_ge(s_xd, b * 8 + 4 + g + 1)
                    apart(sp)
                    sp.dma_start(y_out[bass.ds(b, 1), CH * g:CH * (g + 1), :]
                                 .rearrange("o (t p) d -> p (o t) d", p=P),
                                 x[:, TPC * g:TPC * (g + 1), :]).then_inc(s_out, 16)
                sp.wait_ge(s_out, b * 16 * NQ + 16 * NQ)
                apart(sp)

        @block.gpsimd
        def _(pool):
            pool.memset(ident[:, :], 0.0).then_inc(s_const, 1)
            pool.memset(maskq[:, :], 0.0).then_inc(s_const, 1)
            pool.memset(maskk[:, :], 0.0).then_inc(s_const, 1)
            pool.memset(mhalf[:, :], -0.5).then_inc(s_const, 1)
            pool.memset(xnT[:, :, 0:1], 0.0).then_inc(s_const, 1)
            pool.wait_ge(s_const, 5)
            pool.affine_select(out=ident[:, :], in_=ident[:, :], compare_op=ALU.not_equal, fill=1.0,
                               base=0, pattern=[[-1, P]], channel_multiplier=1).then_inc(s_const, 1)
            pool.affine_select(out=maskq[:, CH - P:CH], in_=maskq[:, CH - P:CH], compare_op=ALU.is_ge, fill=NEG,
                               base=0, pattern=[[-1, P]], channel_multiplier=1).then_inc(s_const, 1)
            pool.affine_select(out=maskk[:, :], in_=maskk[:, :], compare_op=ALU.is_ge, fill=NEG,
                               base=0, pattern=[[1, P]], channel_multiplier=-1).then_inc(s_const, 1)
            pool.wait_ge(s_const, 8)
            pool.tensor_copy(identb[:, :], ident[:, :]).then_inc(s_const, 1)

            with pool.Fori(0, B) as b:
                plinks = [0]

                def plink(ins):
                    plinks[0] += 1
                    ins.then_inc(s_pl, 1)
                    pool.wait_ge(s_pl, b * PLINKS + plinks[0])

                def roots(ln):
                    for g in range(NQ):
                        ts = slice(TPC * g, TPC * (g + 1))
                        pool.wait_ge(s_agg, b * 4 * NQ + ln * NQ + g + 1)
                        apart(pool)
                        pool.tensor_scalar(vare[:, ts], mv[:, ts, 1], EPS, None, ALU.add).then_inc(s_eps, 1)
                        pool.wait_ge(s_eps, b * 4 * NQ + ln * NQ + g + 1)
                        pool.tensor_tensor(rstd[:, ts], vare[:, ts], mhalf[:, ts], ALU.pow).then_inc(s_rstd, 1)

                def read_by_act(stage, e):
                    pool.wait_ge(s_ea, b * EJOBS + FIRST[stage] // 2 + e + 1)

                def add_jobs(stage):
                    for e in range(4):
                        xs = x[:, 4 * e:4 * e + 2, :].rearrange("p t d -> p (t d)")
                        read_by_act(stage, e)
                        pool.tensor_tensor(xs, xs, tmp[:, e % 2, :], ALU.add).then_inc(s_xp, 1)

                roots(0)
                pool.wait_ge(s_rstd, b * 4 * NQ + NQ)
                fills = [(qa[DK0:DK0 + 2, :], 0.0), (ka[DK0:DK0 + 2, :], 1.0),
                         (v0[:, :, DK0:DK0 + 1], 1.0), (ctx0[:, :, DK0:DK0 + 1], 1.0),
                         (stack[KS:P, 0, 1, :], 1.0), (stack[KS:P, 1, 1, :], 1.0)]
                for n, (rows, value) in enumerate(fills):
                    if n > 0:
                        pool.wait_ge(s_fill, b * FILLS + n)
                    apart(pool)
                    pool.memset(rows, value).then_inc(s_fill, 1)
                pool.wait_ge(s_fill, b * FILLS + len(fills))
                add_jobs("WO0")
                roots(1)
                for e in range(4):
                    xs = x[:, 4 * e:4 * e + 2, :]
                    t2 = tmp[:, e % 2, :].rearrange("p (t d) -> p t d", t=2)
                    read_by_act("FFN", e)
                    plink(pool.tensor_tensor(t2, tmp16[:, e % 2, :].rearrange("p (t d) -> p t d", t=2),
                                             bf[:, :].unsqueeze(1).broadcast_to([P, 2, D]), ALU.add))
                    pool.tensor_tensor(xs, xs, t2, ALU.add).then_inc(s_xp, 1)
                roots(2)
                for k, (key, g) in enumerate(QKR):
                    for i in range(TPC):
                        if key == "QK":
                            t = TPC * g + i
                            if i % 2 == 0:
                                pool.wait_ge(s_rt, b * (NT // 2) + t // 2 + 1)
                            else:
                                pool.wait_ge(s_ed, b * EJOBS + (FIRST["QKR"] + TPC * k + i) // 2 + 1)
                            pool.tensor_tensor(roped[:, t % 8, :], qcos[t % 2], qsin[t % 2],
                                               ALU.add).then_inc(s_rope, 1)
                        else:
                            n = 4 * g + i
                            pool.wait_ge(s_mid, b * PJOBS + n + 1)
                            pool.tensor_tensor(parts[:, n % 4, 2, :], resid[n % 4], parts[:, n % 4, 1, :],
                                               ALU.subtract).then_inc(s_lo, 1)
                parts_out(pool, b)
                apart(pool)
                pool.memset(v1[:, :, :, DK1:VW], 1.0).then_inc(s_fill, 1)
                add_jobs("WO1")
                roots(3)
                for n in range(8):
                    q, c = divmod(n, DC)
                    if n % 2 == 0:
                        read_by_act("K", n // 2)
                    else:
                        pool.wait_ge(s_ed, b * EJOBS + FIRST["K"] // 2 + n // 2 + 1)
                    u = tmp[:, (n % 2) * 2 + n // 2 % 2, :]
                    pool.tensor_tensor(kact[:, c, CH * q:CH * (q + 1)], u, u, ALU.mult).then_inc(s_ku, 1)
                for e in range(4):
                    xs = x[:, 4 * e:4 * e + 2, :].rearrange("p t d -> p (t d)")
                    gs = gate[:, 4 * e:4 * e + 2, :].rearrange("p t d -> p (t d)")
                    read_by_act("V", e)
                    plink(pool.tensor_tensor(tmp[:, e % 2, :], tmp[:, e % 2, :], gs, ALU.mult))
                    pool.tensor_tensor(xs, xs, tmp[:, e % 2, :], ALU.add).then_inc(s_xp, 1)
                assert plinks[0] == PLINKS

        @block.scalar
        def _(act):
            def cw(a):
                return a.rearrange("(c p) n -> p c n", p=P)

            for dst, src in [
                (wqk1[:, :, :], cw(w["wqk1"])), (wv1[:, :, :], cw(w["wv1"])), (wo1[:, :, :], cw(w["wo1"])),
                (wr[:, :, :], cw(w["wr"])), (wk[:, :, :], cw(w["wk"])), (wv[:, :, :], cw(w["wv"])),
                (mu[:, :, :], w["mu"]),
            ]:
                act.dma_start(dst, src).then_inc(s_w1, 16)
            act.wait_ge(s_w0, W0)

            with act.Fori(0, B) as b:
                def job(stage, e):
                    j = FIRST[stage] + 2 * e
                    act.wait_ge(s_mm, b * JOBS + j + 1)
                    return bank(j // 2 % 4)

                def turned(stage, dst=xnT, col=1):
                    for g in range(NQ):
                        ps = job(stage, g)
                        apart(act)
                        if dst is xqT:
                            ins = act.activation(dst[:, 0, CH * g:CH * (g + 1)], ps, ACT.Copy, saturate=False)
                        else:
                            ins = act.activation(dst[:, 0, 1 + CH * g:1 + CH * (g + 1)], ps, ACT.Copy)
                        ins.then_inc(s_ea, 1)

                def to_pool(stage, dst, func, used, per_batch, count):
                    for e in range(4):
                        ps = job(stage, e)
                        if e >= 2:
                            act.wait_ge(used, b * per_batch + count(e - 2))
                        elif stage == "V":
                            act.wait_ge(s_ku, b * 8 + 2 * e + 5)
                        act.activation(dst[:, e % 2, :], ps, func).then_inc(s_ea, 1)

                turned("T0")
                for q in range(NQ):
                    ps = job("QK0", q)
                    act.activation(qa[0:DK0, CH * q:CH * (q + 1)], ps[0:DK0, :], ACT.Identity,
                                   bias=bqk0[:, 0:1]).then_inc(s_ea, 1)
                ps = job("V0", 0)
                act.activation(v0[:, 0:NT // 2, 0:DK0], tiles(ps, DK0), ACT.Copy).then_inc(s_ea, 1)
                for k, (q, kb) in enumerate(ORDER):
                    off = span(q, kb)
                    if k >= 4:
                        act.wait_ge(s_v0, b * STEPS + k - 3)
                    act.wait_ge(s_s0, b * STEPS + k + 1)
                    act.activation(probs[:, k % 4, 0:CH - off], bank(k % 4, 0, CH - off), ACT.Exp,
                                   scale=DK0 ** -0.5).then_inc(s_e0, 1)
                for e in range(2):
                    ps = job("CT0", e)
                    act.activation(ctxT[:, 2 * CH * e:2 * CH * e + CH], ps[0:DK0 + 1, :],
                                   ACT.Copy).then_inc(s_ea, 1)
                to_pool("WO0", tmp, ACT.Copy, s_xp, XJOBS, lambda e: e + 1)
                turned("T1", xqT)
                to_pool("FFN", tmp16, ACT.Copy, s_xp, XJOBS, lambda e: 4 + e + 1)
                turned("T2")
                for n, (key, g) in enumerate(QKR):
                    for i in range(0, TPC, 2):
                        ps = job("QKR", (TPC * n + i) // 2)
                        if key == "QK":
                            t = TPC * g + i
                            if t >= 4:
                                act.wait_ge(s_rt, b * (NT // 2) + t // 2 - 1)
                            act.activation(qkc[t // 2 % 2], ps, ACT.Copy).then_inc(s_ea, 1)
                        else:
                            m = 4 * g + i
                            if m >= 4:
                                act.wait_ge(s_pd[m % 4], b * 4 * PJOBS + 16 * (m // 4))
                            act.activation(resid[m % 4], ps, ACT.Copy)
                            act.activation(parts[:, m % 4, 0, :], ps, ACT.Copy).then_inc(s_ea, 1)
                    if key == "RT":
                        for m in range(4 * g, 4 * g + 4):
                            act.wait_ge(s_re, b * PJOBS + m + 1)
                            act.activation(parts[:, m % 4, 1, :], resid[m % 4], ACT.Copy).then_inc(s_mid, 1)
                parts_out(act, b)
                for e in range(4):
                    ps = job("V1", e)
                    act.activation(v1[:, 4 * e:4 * e + 2, :, 0:DK1],
                                   ps.rearrange("p (t h v) -> p t h v", t=2, h=H), ACT.Copy).then_inc(s_ea, 1)
                for kind, item in PLAN1:
                    if kind == "scores":
                        hg, s = item
                        k, pair = divmod(s, 2)
                        off = span(*ORDER[k])
                        at = SUBS * hg + s
                        if at >= 4:
                            act.wait_ge(s_v1, b * NHG * STEPS + at // 2 - 1)
                        act.wait_ge(s_s1, b * NHG * SUBS + at + 1)
                        two = psum[:, 2 * pair * CH:2 * (pair + 1) * CH].rearrange("p (h n) -> p h n", h=2)
                        at = HG * (k % 2) + 2 * pair
                        act.activation(probs[:, at:at + 2, 0:CH - off], two[:, :, 0:CH - off], ACT.Exp,
                                       scale=DK1 ** -0.5).then_inc(s_e1, 1)
                    elif kind == "copy out":
                        hg, q = item
                        oq = NQ * hg + q
                        if oq >= 2:
                            before = ("turned out", divmod(oq - 2, NQ))
                            act.wait_ge(s_p2, b * UNITS1 + UNIT1[before] + 1)
                        k = ORDER.index((q, TPC * (q + 1) - 1))
                        act.wait_ge(s_v1, b * NHG * STEPS + STEPS * hg + k + 1)
                        act.activation(osb[:, oq % 2, :], bank(7), ACT.Copy).then_inc(s_o1, 1)
                turned("AT1")
                to_pool("WO1", tmp, ACT.Copy, s_xp, XJOBS, lambda e: 8 + e + 1)
                turned("T3")
                for e in range(4):
                    ps = job("R", e)
                    act.activation(gate[:, 4 * e:4 * e + 2, :], tiles(ps, D), ACT.Sigmoid).then_inc(s_ea, 1)
                    act.wait_ge(s_ed, b * EJOBS + FIRST["R"] // 2 + e + 1)
                    act.activation(gate[:, 4 * e + 2:4 * e + 4, :], gate[:, 4 * e + 2:4 * e + 4, :],
                                   ACT.Sigmoid).then_inc(s_gate, 1)
                to_pool("K", tmp, ACT.Relu, s_ku, 8, lambda e: 2 * e + 1)
                to_pool("V", tmp, ACT.Copy, s_xp, XJOBS, lambda e: 12 + e + 1)

        @block.vector
        def _(dve):
            chain = [0]

            def then(ins):
                chain[0] += 1
                ins.then_inc(s_wq, 1)
                dve.wait_ge(s_wq, chain[0])

            raw, small, large, pick = (tmp[:, i, :] for i in range(4))
            dve.wait_ge(s_w0, W0)
            dve.tensor_tensor(pick, raw, raw, ALU.mult)
            dve.tensor_scalar(small, raw, 128.0, -128.0, ALU.min, ALU.max)
            then(dve.tensor_scalar(large, raw, 448.0, -448.0, ALU.min, ALU.max))
            dve.tensor_scalar(pick, pick, 128.0 ** 2, None, ALU.is_gt)
            dve.tensor_copy(wf8[:, 0, :], small, saturate=False)
            then(dve.tensor_scalar(wf8[:, 1, :], large, 0.5, None, ALU.mult, saturate=False))
            dve.tensor_copy(small, wf8[:, 0, :])
            then(dve.tensor_scalar(large, wf8[:, 1, :], 2.0, None, ALU.mult))
            then(dve.tensor_tensor(large, large, small, ALU.subtract))
            then(dve.tensor_tensor(large, large, pick, ALU.mult))
            dve.tensor_tensor(wf[:, :, :].rearrange("p c d -> p (c d)"), small, large, ALU.add)
            dve.memset(psum[:, :], 0.0)
            dve.wait_ge(s_w1, W1)
            dve.tensor_scalar(omu[:, :, :], mu[:, :, :], -1.0, 1.0, ALU.mult, ALU.add).then_inc(s_ready, 1)
            dve.wait_ge(s_const, NCONST)

            with dve.Fori(0, B) as b:
                links = [0]

                def link(ins):
                    links[0] += 1
                    ins.then_inc(s_link, 1)
                    dve.wait_ge(s_link, b * LINKS + links[0])

                def norm(ln):
                    def statistics(g):
                        if ln == 0:
                            dve.wait_ge(s_x[g], b * 16 + 16)
                        else:
                            dve.wait_ge(s_xp, b * XJOBS + 4 * (ln - 1) + g + 1)
                            if ln == 2:
                                dve.wait_ge(s_xd, b * 8 + g + 1)
                            else:
                                stage = {1: "WO0", 3: "WO1"}[ln]
                                dve.wait_ge(s_ed, b * EJOBS + FIRST[stage] // 2 + g + 1)
                        for t in range(TPC * g, TPC * (g + 1)):
                            last = dve.bn_stats(stats[:, t, :], x[:, t, :])
                        link(last)
                        apart(dve)
                        for t in range(TPC * g, TPC * (g + 1)):
                            last = dve.bn_aggr(mv[:, t, :], stats[:, t, :])
                        last.then_inc(s_agg, 1)

                    def scale(g):
                        dve.wait_ge(s_rstd, b * 4 * NQ + ln * NQ + g + 1)
                        for t in range(TPC * g, TPC * (g + 1)):
                            last = dve.tensor_scalar(xn[:, t, :], x[:, t, :], mv[:, t, 0:1], rstd[:, t:t + 1],
                                                     ALU.subtract, ALU.mult)
                        last.then_inc(s_norm, 1)

                    statistics(0)
                    for g in range(1, NQ):
                        statistics(g)
                        scale(g - 1)
                    scale(NQ - 1)

                def job(stage, e):
                    j = FIRST[stage] + 2 * e + 1
                    dve.wait_ge(s_mm, b * JOBS + j + 1)
                    return bank(4 + j // 2 % 4)

                def turned(stage, dst=xnT):
                    for g in range(NQ):
                        ps = job(stage, g)
                        apart(dve)
                        col = 0 if dst is xqT else 1
                        kind = {"saturate": False} if dst is xqT else {}
                        dve.tensor_copy(dst[:, 1, col + CH * g:col + CH * (g + 1)], ps, **kind).then_inc(s_ed, 1)

                def add_jobs(stage):
                    for e in range(4):
                        ps = job(stage, e)
                        xs = x[:, 4 * e + 2:4 * e + 4, :]
                        dve.tensor_tensor(xs, tiles(ps, D), xs, ALU.add).then_inc(s_ed, 1)

                norm(0)
                turned("T0")
                for q in range(NQ):
                    ps = job("QK0", q)
                    dve.tensor_scalar(ka[0:DK0, CH * q:CH * (q + 1)], ps[0:DK0, :], bqk0[:, 1:2], None,
                                      ALU.add).then_inc(s_ed, 1)
                ps = job("V0", 0)
                dve.tensor_copy(v0[:, NT // 2:NT, 0:DK0], tiles(ps, DK0)).then_inc(s_ed, 1)

                def read_scores(ps, n, diagonal, out, slot):
                    if diagonal:
                        apart(dve)
                        ins = dve.tensor_tensor_reduce(junk[:, slot, 0:n], ps, maskq[:, CH - n:CH], 1.0, -3e38,
                                                       ALU.add, ALU.max, out)
                    else:
                        ins = dve.tensor_reduce(out, ps, AX.X, ALU.max)
                    return ins

                def copy_out(oq, rows):
                    dve.tensor_copy(osb[0:rows, oq % 2, :], bank(6 + oq % 2, rows=rows)).then_inc(s_oe, 1)

                for kind, n in plan0():
                    if kind == "max":
                        i, c = MAX0[n]
                        ps = bank(4 + n % 2)
                        if i is None:
                            dve.wait_ge(s_m1, b * UNITS0 + n)
                            ts = slice(TPC * c, TPC * (c + 1))
                            dve.tensor_reduce(nmax0[:, ts], mx0[:, ts, 0:c + 1], AX.X, ALU.max,
                                              negate=True).then_inc(s_nm0, 1)
                            dve.wait_ge(s_p1, b * UNITS0 + n + 1)
                            if c >= 1:
                                dve.wait_ge(s_row0, b * 16 * NQ + 16 * c)
                            dve.tensor_copy(nmaxT0[:, :], ps[0:TPC, 0:P]).then_inc(s_m1, 1)
                        else:
                            width = CH if c < i // TPC else (i % TPC + 1) * P
                            if n >= 4:
                                dve.wait_ge(s_m1, b * UNITS0 + n - 3)
                            dve.wait_ge(s_p1, b * UNITS0 + n + 1)
                            read_scores(ps[:, 0:width], width, c == i // TPC, mx0[:, i, c:c + 1],
                                        n % 4).then_inc(s_m1, 1)
                    elif kind == "copy out":
                        dve.wait_ge(s_v0, b * STEPS + ORDER.index((n, TPC * (n + 1) - 1)) + 1)
                        copy_out(n, DK0 + 1)
                    elif kind == "turn":
                        dve.wait_ge(s_ot, b * NQ + n + 1)
                        turned_o = tiles(bank(6 + n % 2), P)
                        ts = slice(TPC * n, TPC * (n + 1))
                        link(dve.reciprocal(rec[:, :, 0], turned_o[:, :, DK0]))
                        link(dve.tensor_tensor(ctx0[:, ts, 0:DK0], turned_o[:, :, 0:DK0],
                                               rec[:, :, 0:1].broadcast_to([P, TPC, DK0]), ALU.mult))
                        dve.tensor_tensor(ctx0[:, ts, 0:DK0], ctx0[:, ts, 0:DK0],
                                          bv0[:, :].unsqueeze(1).broadcast_to([P, TPC, DK0]),
                                          ALU.add).then_inc(s_oc, 1)
                for e in range(2):
                    ps = job("CT0", e)
                    dve.tensor_copy(ctxT[:, CH * (2 * e + 1):CH * (2 * e + 2)], ps[0:DK0 + 1, :]).then_inc(s_ed, 1)
                add_jobs("WO0")
                norm(1)
                turned("T1", xqT)
                for e in range(4):
                    ps = job("FFN", e)
                    xs = x[:, 4 * e + 2:4 * e + 4, :]
                    t16, t32 = tiles(tmp16[:, 2 + e % 2, :], D), tiles(tmp[:, 2 + e % 2, :], D)
                    dve.tensor_copy(t16, tiles(ps, D)).then_inc(s_ed, 1)
                    dve.wait_ge(s_ed, b * EJOBS + FIRST["FFN"] // 2 + e + 1)
                    link(dve.tensor_tensor(t32, t16, bf[:, :].unsqueeze(1).broadcast_to([P, 2, D]), ALU.add))
                    dve.tensor_tensor(xs, xs, t32, ALU.add).then_inc(s_xd, 1)
                norm(2)
                turned("T2")
                for n, (key, g) in enumerate(QKR):
                    for i in range(TPC):
                        if key == "QK":
                            t = TPC * g + i
                            if i % 2 == 0:
                                dve.wait_ge(s_ea, b * EJOBS + (FIRST["QKR"] + TPC * n + i) // 2 + 1)
                                src = qkc[t // 2 % 2]
                            else:
                                src = job("QKR", (TPC * n + i) // 2)
                            if t >= 2:
                                dve.wait_ge(s_rope, b * NT + t - 1)
                            src = src.rearrange("p (h d) -> p h d", d=DK1)
                            half = DK1 // 2
                            to_cos = qcos[t % 2].rearrange("p (h d) -> p h d", d=DK1)
                            to_sin = qsin[t % 2].rearrange("p (h d) -> p h d", d=DK1)
                            cs = cos[:, t, :].unsqueeze(1)
                            sn = sin[:, t, :].unsqueeze(1)
                            dve.tensor_tensor(to_cos, src, cs.broadcast_to([P, 2 * H, DK1]), ALU.mult)
                            dve.tensor_tensor(to_sin[:, :, 0:half], src[:, :, half:DK1],
                                              sn[:, :, 0:half].broadcast_to([P, 2 * H, half]), ALU.mult)
                            ins = dve.tensor_tensor(to_sin[:, :, half:DK1], src[:, :, 0:half],
                                                    sn[:, :, half:DK1].broadcast_to([P, 2 * H, half]), ALU.mult)
                            ins.then_inc(s_ed if i % 2 else s_rt, 1)
                        else:
                            m = 4 * g + i
                            if i % 2 == 1:
                                ps = job("QKR", (TPC * n + i) // 2)
                                if m >= 4:
                                    dve.wait_ge(s_pd[m % 4], b * 4 * PJOBS + 16 * (m // 4))
                                dve.tensor_copy(resid[m % 4], ps)
                                dve.tensor_copy(parts[:, m % 4, 0, :], ps).then_inc(s_ed, 1)
                            dve.wait_ge(s_ed if i % 2 else s_ea,
                                        b * EJOBS + (FIRST["QKR"] + TPC * n + i) // 2 + 1)
                            dve.tensor_tensor(resid[m % 4], resid[m % 4], parts[:, m % 4, 0, :],
                                              ALU.subtract).then_inc(s_re, 1)
                parts_out(dve, b)
                for e in range(4):
                    ps = job("V1", e)
                    dve.tensor_copy(v1[:, 4 * e + 2:4 * e + 4, :, 0:DK1].rearrange("p t h v -> p (t h) v"),
                                    tiles(ps, DK1)).then_inc(s_ed, 1)

                for kind, item in PLAN1:
                    if (kind, item) in UNIT1:
                        at = UNIT1[kind, item]
                        ps = bank(4 + at % MB)
                    if kind == "max":
                        hg, i, c, h = item
                        width = CH if c < i // TPC else (i % TPC + 1) * P
                        if at >= 4:
                            dve.wait_ge(s_m2, b * UNITS1 + at - 3)
                        dve.wait_ge(s_p2, b * UNITS1 + at + 1)
                        read_scores(ps[:, 0:width], width, c == i // TPC,
                                    mx1[:, h, i, c:c + 1], at % 4).then_inc(s_m2, 1)
                    elif kind == "minus max":
                        hg, q = item
                        oq = NQ * hg + q
                        dve.wait_ge(s_m2, b * UNITS1 + at + 1)
                        if oq >= 1:
                            before = ("turned max", divmod(oq - 1, NQ))
                            dve.wait_ge(s_p2, b * UNITS1 + UNIT1[before] + 1)
                        link(dve.tensor_reduce(nmax1[:, :].rearrange("p (h t) -> p h t", h=HG),
                                               mx1[:, :, TPC * q:TPC * (q + 1), 0:q + 1],
                                               AX.X, ALU.max, negate=True))
                        minus = nmax1[:, :].rearrange("p (h t) -> p h t", h=HG)
                        link(dve.tensor_copy(nmaxb[:, :, 0, :], minus))
                        dve.tensor_tensor(nmaxb[:, :, 1, :], minus, nmaxb[:, :, 0, :],
                                          ALU.subtract).then_inc(s_nm1, 1)
                    elif kind == "turned max":
                        oq = NQ * item[0] + item[1]
                        if oq >= 2:
                            dve.wait_ge(s_row1[oq % 2], b * (ROWS * OUTS // 2) + ROWS * (oq // 2))
                        dve.wait_ge(s_p2, b * UNITS1 + at + 1)
                        dve.tensor_copy(nmaxT1[:, oq % 2, :],
                                        ps.bitcast(BF16)[0:HG * MAXROWS * TPC, 0:P]).then_inc(s_m2, 1)
                    elif kind == "turned out":
                        hg, q = item
                        dve.wait_ge(s_m2, b * UNITS1 + at)
                        dve.wait_ge(s_p2, b * UNITS1 + at + 1)
                        turned_o = ps.rearrange("p (t h v) -> p t h v", t=TPC, h=HG)
                        link(dve.reciprocal(rec[:, :, :], turned_o[:, :, :, DK1]))
                        cols = att[:, TPC * q:TPC * (q + 1), HG * DK1 * hg:HG * DK1 * (hg + 1)]
                        dve.tensor_tensor(cols.rearrange("p t (h v) -> p t h v", h=HG),
                                          turned_o[:, :, :, 0:DK1],
                                          rec[:, :, :].unsqueeze(3).broadcast_to([P, TPC, HG, DK1]),
                                          ALU.mult).then_inc(s_m2, 1)

                turned("AT1")
                add_jobs("WO1")
                norm(3)
                turned("T3")
                for g in range(NQ):
                    dve.wait_ge(s_ea, b * EJOBS + FIRST["T3"] // 2 + g + 1)
                    dve.wait_ge(s_ed, b * EJOBS + FIRST["T3"] // 2 + g + 1)
                    ts = slice(CH * g, CH * (g + 1))
                    pairs = [(to, i, c) for i, to in enumerate((xr, xk)) for c in range(DC)]
                    for to, i, c in pairs:
                        last = dve.tensor_scalar(to[:, c, ts], xnT[:, c, ts], omu[:, i, c:c + 1], None, ALU.mult)
                    link(last)
                    for to, i, c in pairs:
                        last = dve.scalar_tensor_tensor(out=to[:, c, ts], in0=xnT[:, c, 1 + CH * g:1 + CH * (g + 1)],
                                                        scalar=mu[:, i, c:c + 1], in1=to[:, c, ts],
                                                        op0=ALU.mult, op1=ALU.add)
                    last.then_inc(s_mix, 1)
                for e in range(4):
                    ps = job("R", e)
                    dve.tensor_copy(gate[:, 4 * e + 2:4 * e + 4, :], tiles(ps, D)).then_inc(s_ed, 1)
                for e in range(4):
                    ps = job("K", e)
                    if e >= 2:
                        dve.wait_ge(s_ku, b * 8 + 2 * e - 2)
                    dve.tensor_scalar(tmp[:, 2 + e % 2, :], ps, 0.0, None, ALU.max).then_inc(s_ed, 1)
                for e in range(4):
                    ps = job("V", e)
                    dve.wait_ge(s_gate, b * 4 + e + 1)
                    if e < 2:
                        dve.wait_ge(s_ku, b * 8 + 2 * e + 6)
                    xs = x[:, 4 * e + 2:4 * e + 4, :]
                    t32 = tiles(tmp[:, 2 + e % 2, :], D)
                    dve.tensor_tensor(t32, tiles(ps, D), gate[:, 4 * e + 2:4 * e + 4, :], ALU.mult).then_inc(s_ed, 1)
                    dve.wait_ge(s_ed, b * EJOBS + FIRST["V"] // 2 + e + 1)
                    dve.tensor_tensor(xs, xs, t32, ALU.add).then_inc(s_xd, 1)
                assert links[0] == LINKS, (links[0], LINKS)

        @block.tensor
        def _(pe):
            pe.wait_ge(s_w0, W0)
            pe.wait_ge(s_const, NCONST)
            pe.wait_ge(s_ready, 1)

            with pe.Fori(0, B) as b:
                def job(stage, n):
                    j = FIRST[stage] + n
                    e = j // 2
                    if e >= 4:
                        pe.wait_ge(s_ed if j % 2 else s_ea, b * EJOBS + e - 3)
                    return bank((4 if j % 2 else 0) + e % 4)

                def jobs_read(stage):
                    pe.wait_ge(s_ea, b * EJOBS + FIRST[stage] // 2)
                    pe.wait_ge(s_ed, b * EJOBS + FIRST[stage] // 2)

                def turn(stage, src, ready):
                    for g in range(NQ):
                        ready(g)
                        for c in range(DC):
                            ps = job(stage, 2 * g + c)
                            for i in range(TPC):
                                last = pe.transpose(ps[:, i * P:(i + 1) * P],
                                                    src[:, TPC * g + i, c * P:(c + 1) * P], ident[:, :])
                            last.then_inc(s_mm, 1)

                def normalised(ln):
                    return lambda g: pe.wait_ge(s_norm, b * 4 * NQ + ln * NQ + g + 1)

                def turned(stage, g):
                    pe.wait_ge(s_ea, b * EJOBS + FIRST[stage] // 2 + g + 1)
                    pe.wait_ge(s_ed, b * EJOBS + FIRST[stage] // 2 + g + 1)

                def by_tiles(stage, lhs, rhs, ready, chunks=DC):
                    for n in range(NT // 2):
                        if n % 2 == 0:
                            ready(n // 2)
                        ps = job(stage, n)
                        if stage == "FFN":
                            apart(pe)
                        for i in range(2):
                            for c in range(chunks):
                                last = pe.matmul(ps[:, i * D:(i + 1) * D], lhs(c, 2 * n + i), rhs(c),
                                                 start=(c == 0), stop=(c == chunks - 1))
                        last.then_inc(s_mm, 1)

                def tok(c, t):
                    return xnT[:, c, 1 + P * t:1 + P * (t + 1)]

                turn("T0", xn, normalised(0))
                for n in range(2 * NQ):
                    q, side = divmod(n, 2)
                    if side == 0:
                        turned("T0", q)
                    ps = job("QK0", n)
                    for c in range(DC):
                        last = pe.matmul(ps[0:DK0, :], wqk0[:, c, side * DK0:(side + 1) * DK0],
                                         xnT[:, c, 1 + CH * q:1 + CH * (q + 1)], start=(c == 0), stop=(c == DC - 1))
                    last.then_inc(s_mm, 1)
                for n in range(2):
                    ps = job("V0", n)
                    for i in range(NT // 2):
                        for c in range(DC):
                            last = pe.matmul(ps[:, i * DK0:(i + 1) * DK0], tok(c, NT // 2 * n + i), wv0[:, c, :],
                                             start=(c == 0), stop=(c == DC - 1))
                    last.then_inc(s_mm, 1)

                jobs_read("CT0")
                pe.wait_ge(s_fill, b * FILLS + 4)
                for kind, n in plan0():
                    if kind == "max":
                        i, c = MAX0[n]
                        if n >= 2:
                            pe.wait_ge(s_m1, b * UNITS0 + n - 1)
                        ps = bank(4 + n % 2)
                        if i is None:
                            pe.wait_ge(s_nm0, b * NQ + c + 1)
                            pe.transpose(ps[0:TPC, 0:P], nmax0[:, TPC * c:TPC * (c + 1)], ident[:, :]).then_inc(s_p1, 1)
                        else:
                            width = CH if c < i // TPC else (i % TPC + 1) * P
                            pe.matmul(ps[:, 0:width], qa[0:DK0 + 1, P * i:P * (i + 1)],
                                      ka[0:DK0 + 1, CH * c:CH * c + width], start=True, stop=True).then_inc(s_p1, 1)
                    elif kind == "scores":
                        q, kb = ORDER[n]
                        off = span(q, kb)
                        if kb == 0:
                            pe.wait_ge(s_row0, b * 16 * NQ + 16 * (q + 1))
                        if n >= 4:
                            pe.wait_ge(s_e0, b * STEPS + n - 3)
                        diagonal = kb >= TPC * q
                        ins = pe.matmul(bank(n % 4, 0, CH - off), ka[0:DK0 + 2, P * kb:P * (kb + 1)],
                                        qa[0:DK0 + 2, CH * q + off:CH * (q + 1)], start=True, stop=not diagonal)
                        if diagonal:
                            ins = pe.matmul(bank(n % 4, 0, P), identb[:, :], maskk[:, :], start=False, stop=True)
                        ins.then_inc(s_s0, 1)
                    elif kind == "values":
                        q, kb = ORDER[n]
                        off = span(q, kb)
                        if kb == 0 and q >= 2:
                            pe.wait_ge(s_oc, b * NQ + q - 1)
                        pe.wait_ge(s_e0, b * STEPS + n + 1)
                        pe.matmul(bank(6 + q % 2, off, CH, rows=DK0 + 1), v0[:, kb, :], probs[:, n % 4, 0:CH - off],
                                  start=(kb == 0), stop=last_block(n)).then_inc(s_v0, 1)
                    elif kind == "turn":
                        pe.wait_ge(s_oe, b * NQ + n + 1)
                        for i in range(TPC):
                            ins = pe.transpose(bank(6 + n % 2, P * i, P * i + DK0 + 1),
                                               osb[0:DK0 + 1, n % 2, P * i:P * (i + 1)],
                                               ident[0:DK0 + 1, 0:DK0 + 1])
                        ins.then_inc(s_ot, 1)
                pe.wait_ge(s_oc, b * NQ + NQ)
                for n in range(NQ):
                    ps = job("CT0", n)
                    apart(pe)
                    for i in range(TPC):
                        last = pe.transpose(ps[0:DK0 + 1, P * i:P * (i + 1)], ctx0[:, TPC * n + i, :], ident[:, :])
                    last.then_inc(s_mm, 1)

                def context(g):
                    pe.wait_ge(s_ed if g % 2 else s_ea, b * EJOBS + FIRST["CT0"] // 2 + g // 2 + 1)

                by_tiles("WO0", lambda c, t: ctxT[:, P * t:P * (t + 1)], lambda c: wo0[:, :], context, 1)

                turn("T1", xn, normalised(1))
                by_tiles("FFN", lambda c, t: xqT[:, c, P * t:P * (t + 1)], lambda c: wf[:, c, :],
                         lambda g: turned("T1", g))

                turn("T2", xn, normalised(2))
                for n, (key, g) in enumerate(QKR):
                    if key == "QK":
                        turned("T2", g)
                    else:
                        pe.wait_ge(s_rope, b * NT + TPC * (g + 1))
                    for i in range(TPC):
                        ps = job("QKR", TPC * n + i)
                        if key == "QK":
                            for c in range(DC):
                                last = pe.matmul(ps, tok(c, TPC * g + i), wqk1[:, c, :],
                                                 start=(c == 0), stop=(c == DC - 1))
                        else:
                            for t in range(TPC):
                                last = pe.transpose(ps[:, P * t:P * (t + 1)],
                                                    roped[:, (TPC * g + t) % 8, P * i:P * (i + 1)], ident[:, :])
                        last.then_inc(s_mm, 1)
                by_tiles("V1", tok, lambda c: wv1[:, c, :], lambda g: None)

                jobs_read("AT1")
                pe.wait_ge(s_fill, b * FILLS + FILLS)
                for kind, item in PLAN1:
                    if (kind, item) in UNIT1:
                        at = UNIT1[kind, item]
                        if at >= MB:
                            pe.wait_ge(s_m2, b * UNITS1 + at - MB + 1)
                        ps = bank(4 + at % MB)
                    if kind == "max":
                        hg, i, c, h = item
                        if hg == 0 and (i % TPC, c, h) == (0, 0, 0):
                            pe.wait_ge(s_first[i // TPC], b * STK + STK)
                        elif hg > 0 and (i, c, h) == (0, 0, 0):
                            pe.wait_ge(s_stk[hg % 2], b * (STK * STKS[hg % 2]) + STK * (hg // 2 + hg % 2))
                        width = CH if c < i // TPC else (i % TPC + 1) * P
                        pe.matmul(ps[:, 0:width], qs[hg % 2][0:KS, h, P * i:P * (i + 1)],
                                  ks[hg % 2][0:KS, h, CH * c:CH * c + width],
                                  start=True, stop=True).then_inc(s_p2, 1)
                    elif kind == "turned max":
                        pe.wait_ge(s_nm1, b * OUTS + NQ * item[0] + item[1] + 1)
                        pe.transpose(ps.bitcast(BF16)[0:HG * MAXROWS * TPC, 0:P],
                                     nmaxb[:, :, :, :].rearrange("p h r t -> p (h r t)"),
                                     identb[:, :]).then_inc(s_p2, 1)
                    elif kind == "turned out":
                        oq = NQ * item[0] + item[1]
                        pe.wait_ge(s_o1, b * OUTS + oq + 1)
                        for i in range(TPC):
                            ins = pe.transpose(ps[:, P * i:P * (i + 1)], osb[:, oq % 2, P * i:P * (i + 1)],
                                               ident[:, :])
                        ins.then_inc(s_p2, 1)
                    elif kind == "scores":
                        hg, s = item
                        k, pair = divmod(s, 2)
                        q, kb = ORDER[k]
                        off = span(q, kb)
                        at = SUBS * hg + s
                        oq = NQ * hg + q
                        if kb == 0 and pair == 0:
                            pe.wait_ge(s_row1[oq % 2], b * (ROWS * OUTS // 2) + ROWS * (oq // 2 + 1))
                        if at >= 2:
                            pe.wait_ge(s_e1, b * NHG * SUBS + at - 1)
                        diagonal = kb >= TPC * q
                        rows = slice(0, KS + MAXROWS)
                        for h in range(2 * pair, 2 * pair + 2):
                            ins = pe.matmul(bank(h, 0, CH - off), ks[hg % 2][rows, h, P * kb:P * (kb + 1)],
                                            qs[hg % 2][rows, h, CH * q + off:CH * (q + 1)],
                                            start=True, stop=not diagonal)
                            if diagonal:
                                ins = pe.matmul(bank(h, 0, P), identb[:, :], maskk[:, :], start=False, stop=True)
                        ins.then_inc(s_s1, 1)
                    elif kind == "values":
                        hg, k = item
                        q, kb = ORDER[k]
                        off = span(q, kb)
                        oq = NQ * hg + q
                        if kb == 0 and oq >= 1:
                            pe.wait_ge(s_o1, b * OUTS + oq)
                        pe.wait_ge(s_e1, b * NHG * SUBS + SUBS * hg + 2 * k + 2)
                        for h in range(HG):
                            ins = pe.matmul(bank(7, off, CH, rows=VW, row=32 * h),
                                            v1[:, kb, HG * hg + h, :], probs[:, HG * (k % 2) + h, 0:CH - off],
                                            start=(kb == 0), stop=last_block(k))
                        ins.then_inc(s_v1, 1)
                turn("AT1", att, lambda g: pe.wait_ge(s_m2, b * UNITS1 + UNITS1))
                by_tiles("WO1", tok, lambda c: wo1[:, c, :], lambda g: turned("AT1", g))

                turn("T3", xn, normalised(3))
                pe.wait_ge(s_w1, W1)
                by_tiles("R", lambda c, t: xr[:, c, P * t:P * (t + 1)], lambda c: wr[:, c, :],
                         lambda g: pe.wait_ge(s_mix, b * NQ + g + 1))
                for n in range(2 * NQ):
                    q, half = divmod(n, DC)
                    ps = job("K", n)
                    for c in range(DC):
                        last = pe.matmul(ps, wk[:, c, P * half:P * (half + 1)], xk[:, c, CH * q:CH * (q + 1)],
                                         start=(c == 0), stop=(c == DC - 1))
                    last.then_inc(s_mm, 1)
                by_tiles("V", lambda c, t: kact[:, c, P * t:P * (t + 1)], lambda c: wv[:, c, :],
                         lambda g: pe.wait_ge(s_ku, b * 8 + 2 * (g + 1)))


def rope_tables():
    theta = (np.float32(1.0) / np.float32(10000.0) ** (np.arange(0, DK1, 2, dtype=np.float32) / np.float32(DK1)))
    angle = np.outer(np.arange(T, dtype=np.float32), theta.astype(np.float32)).astype(np.float32)
    angle = np.concatenate([angle, angle], axis=-1)
    sign = np.where(np.arange(DK1) < DK1 // 2, np.float32(-1), np.float32(1))
    return np.cos(angle).astype(np.float32), (np.sin(angle) * sign).astype(np.float32)


def arrays(inputs):
    a = {k.replace("L0_attn_", "a0_").replace("L0_ffn_", "f0_").replace("L1_attn_", "a1_").replace("L1_ffn_", "f1_"):
         np.asarray(v) for k, v in inputs.items()}
    c, s = rope_tables()
    w = {
        "wqk0": np.concatenate([a["a0_Wq"], a["a0_Wk"]]).T, "wv0": a["a0_Wv"].T, "wo0": a["a0_Wo"].T,
        "bqk0": np.stack([a["a0_bq"], a["a0_bk"]]).T, "bv0": a["a0_bv"], "bo0": a["a0_bo"],
        "wf": a["f0_weight"].T, "bf": a["f0_bias"],
        "wqk1": np.concatenate([a["a1_W_Q"], a["a1_W_K"]]).T, "wv1": a["a1_W_V"].T, "wo1": a["a1_W_O"].T,
        "wr": a["f1_W_r"].T, "wk": a["f1_W_k"].T, "wv": a["f1_W_v"].T,
        "mu": np.stack([a["f1_mu_r"], a["f1_mu_k"]]).reshape(2, DC, P).transpose(2, 0, 1), "cos": c, "sin": s,
    }
    return a["a0_y_all"], {k: np.ascontiguousarray(v) for k, v in w.items()}


def kernel(**inputs):
    import concourse.bacc as bacc
    from concourse.bass_utils import run_bass_kernel_spmd

    nc = bacc.Bacc("TRN2", target_bir_lowering=False, num_devices=1)
    x, w = arrays(inputs)
    x_in = nc.dram_tensor("x_in", x.shape, F32, kind="ExternalInput").ap()
    aps = {k: nc.dram_tensor("w_" + k, v.shape, F32, kind="ExternalInput").ap() for k, v in w.items()}
    y = nc.dram_tensor("y_out", (B, T, D), F32, kind="ExternalOutput").ap()
    build(nc, x_in, y, aps)
    r = run_bass_kernel_spmd(nc, [{"x_in": x, **{"w_" + k: v for k, v in w.items()}}], core_ids=[0])
    return r.results[0]["y_out"]
```

```python
from contextlib import ExitStack

import numpy as np

import concourse.bass as bass
from concourse import mybir

ALU = mybir.AluOpType
ACT = mybir.ActivationFunctionType
AX = mybir.AxisListType
F32 = mybir.dt.float32
F16 = mybir.dt.float16
BF16 = mybir.dt.bfloat16
FP8 = mybir.dt.float8e4

P = 128
B, T, D = 4, 2048, 256
NT = T // P
CH = 512
NQ = T // CH
TPC = CH // P
DC = D // P
EPS = 1e-5
NEG = -1e38

DK0 = 64
H, DK1 = 16, 16
HG = 4
NHG = H // HG
VW = DK1 + 1
PARTS = 3
TERMS = [(0, 0), (0, 1), (0, 2), (1, 0), (1, 1), (2, 0)]
KS = len(TERMS) * DK1
MAXROWS = 2

STAGES = [("T0", 8), ("QK0", 8), ("V0", 2), ("CT0", 4), ("WO0", 8), ("T1", 8), ("FFN", 8), ("T2", 8),
          ("QKR", 32), ("AT1", 8), ("WO1", 8), ("T3", 8), ("R", 8), ("K", 8), ("V", 8)]
FIRST = {}
_n = 0
for _name, _count in STAGES:
    FIRST[_name] = _n
    _n += _count
JOBS = _n
EJOBS = JOBS // 2

QKR = [("QK", 0), ("QK", 1), ("RT", 0), ("QK", 2), ("RT", 1), ("QK", 3), ("RT", 2), ("RT", 3)]
QKR_AT = {key: FIRST["QKR"] + TPC * n for n, key in enumerate(QKR)}

UNITS0 = sum(TPC * (q + 1) + 1 for q in range(NQ))
STEPS = sum(TPC * (q + 1) for q in range(NQ))
SUBS = 2 * STEPS
MB = 3


def max_units0():
    units = []
    for q in range(NQ):
        units += [(i, c) for i in range(TPC * q, TPC * (q + 1)) for c in range(q + 1)] + [(None, q)]
    return units


def steps():
    return [(q, kb) for q in range(NQ) for kb in range(TPC * (q + 1))]


def span(q, kb):
    return max(0, kb - TPC * q) * P


MAX0, ORDER = max_units0(), steps()
assert len(MAX0) == UNITS0 and len(ORDER) == STEPS


def last_block(k):
    q, kb = ORDER[k]
    return kb == TPC * (q + 1) - 1


def plan0():
    plan, unit = [], 0
    for k in range(STEPS + 2):
        if k < STEPS:
            q, kb = ORDER[k]
            if kb == 0:
                for ahead in range(0 if q == 0 else q + 1, min(q + 2, NQ)):
                    while MAX0[unit] != (None, ahead):
                        plan.append(("max", unit))
                        unit += 1
                    plan.append(("max", unit))
                    unit += 1
            plan.append(("scores", k))
        if k >= 2:
            plan.append(("values", k - 2))
            q, kb = ORDER[k - 2]
            if last_block(k - 2):
                plan.append(("copy out", q))
            if q > 0 and kb == 2:
                plan.append(("turn", q - 1))
    plan.append(("turn", NQ - 1))
    return plan


def plan1():
    first, second = [], [("project", (0, t)) for t in range(NT)]
    for g in range(NHG):
        for q in range(NQ):
            block = [("max", (g, i, c, h)) for i in range(TPC * q, TPC * (q + 1))
                     for c in range(q + 1) for h in range(HG)]
            if g + q > 0:
                block.insert(2, ("turned max", divmod(NQ * g + q - 1, NQ)))
            first += block + [("minus max", (g, q))]
    first.append(("turned max", (NHG - 1, NQ - 1)))
    for n in range(NHG * STEPS + 1):
        if n < NHG * STEPS:
            g, k = divmod(n, STEPS)
            second += [("scores", (g, 2 * k)), ("scores", (g, 2 * k + 1))]
        if n > 0:
            second.append(("values", divmod(n - 1, STEPS)))

    hop = 0.1
    plan, read, weights, rows = [], [], [], {}
    loaded = {0: 0.0, 1: 20.0}
    tensor = vector = scalar = copied = 0.0
    n1 = n2 = 0

    def unit_width(item):
        if item[0] != "max":
            return P * TPC
        _, i, c, _ = item[1]
        return CH if c < i // TPC else (i % TPC + 1) * P

    def unit(item):
        nonlocal tensor, vector
        plan.append(item)
        size = unit_width(item) / CH
        free = read[-MB] + hop if len(read) >= MB else 0.0
        tensor = max(tensor, free) + {"turned out": 0.86, "turned max": 0.11}.get(item[0], 0.216 * size)
        vector = max(vector, tensor + hop) + {"turned out": 0.6, "turned max": 0.2}.get(item[0], 0.08 + 0.533 * size)
        read.append(vector)
        if item[0] == "turned max":
            rows[item[1]] = vector + 6.0

    while n2 < len(second):
        unit_at = step_at = 1e9
        if n1 < len(first):
            free = read[-MB] + hop if len(read) >= MB else 0.0
            unit_at = max(tensor, free, loaded.get(first[n1][1][0], 1e9))
        kind, (g, s) = second[n2]
        k = s // 2 if kind == "scores" else 0 if kind == "project" else s
        q, kb = ORDER[k]
        size = (CH - span(q, kb)) / CH
        if kind == "scores":
            done = weights[-2] + hop if len(weights) >= 2 else scalar + hop
            step_at = max(tensor, done, rows.get((g, q), 1e9))
        elif kind == "project":
            step_at = tensor
        else:
            step_at = max(tensor, weights[2 * (STEPS * g + k) + 1] + hop, copied if kb == 0 else 0.0)
        if unit_at < 1e9 and (unit_at < tensor + 0.05 and vector - tensor < EAGER or unit_at < step_at - 0.05):
            tensor = unit_at
            item = first[n1]
            n1 += 1
            if item[0] == "minus max":
                plan.append(item)
                vector += 0.5
            else:
                unit(item)
            continue
        n2 += 1
        plan.append((kind, (g, s)))
        if kind == "project":
            tensor = step_at + 0.86
            scalar = max(scalar, tensor + hop) + 0.25
        elif kind == "scores":
            tensor = step_at + 0.44 * size + (0.11 if kb >= TPC * q else 0.0)
            scalar = max(scalar, tensor + hop) + 0.05 + 0.853 * size
            weights.append(scalar)
            if s == SUBS - 1:
                loaded[g + 2] = tensor + 18.0
        else:
            tensor = step_at + 0.92 * size
            if last_block(k):
                plan.append(("copy out", (g, q)))
                scalar = max(scalar, tensor + hop) + 0.48
                copied = scalar + hop
            if kb == 2 and (g, q) != (0, 0):
                unit(("turned out", divmod(NQ * g + q - 1, NQ)))
    plan.append(("turned out", (NHG - 1, NQ - 1)))
    assert n1 == len(first)
    return plan


EAGER = 0.9
PLAN1 = plan1()
UNIT1 = {item: n for n, item in enumerate(x for x in PLAN1 if x[0] in ("max", "turned max", "turned out"))}
UNITS1 = len(UNIT1)


def build(nc, x_in, y_out, w):
    ctx = ExitStack()
    with ctx:
        def sb(name, shape, dt):
            return ctx.enter_context(nc.sbuf_tensor(name, shape, dt))

        def sem(name):
            return ctx.enter_context(nc.semaphore(name))

        psum = ctx.enter_context(nc.psum_tensor("psum", [P, 8 * CH], F32))

        def bank(n, lo=0, hi=CH, rows=P, row=0):
            return psum[row:row + rows, n * CH + lo:n * CH + hi]

        x = sb("x", [P, NT, D], F32)
        xn = sb("xn", [P, NT, D], F32)
        xnT = sb("xnT", [P, DC, 1 + T], F32)
        xqT = sb("xqT", [P, DC, T], FP8)
        stats = sb("stats", [P, NT, 6], F32)
        mv = sb("mv", [P, NT, 2], F32)
        vare = sb("vare", [P, NT], F32)
        rstd = sb("rstd", [P, NT], F32)
        shift = sb("shift", [P, NT], F32)
        mhalf = sb("mhalf", [P, NT], F32)
        ident = sb("ident", [P, P], F32)
        identb = sb("identb", [P, P], BF16)
        maskq = sb("maskq", [P, CH], BF16)
        maskk = sb("maskk", [P, P], BF16)
        cos = sb("cos", [P, NT, DK1], F32)
        sin = sb("sin", [P, NT, DK1], F32)
        wqk0 = sb("wqk0", [P, DC, 2 * DK0], F32)
        wv0 = sb("wv0", [P, DC, DK0], F32)
        wo0 = sb("wo0", [DK0 + 1, D], F32)
        bqk0 = sb("bqk0", [DK0, 2], F32)
        bv0 = sb("bv0", [P, DK0], F32)
        wf = sb("wf", [P, DC, D], BF16)
        wf8 = sb("wf8", [P, 2, DC * D], FP8)
        bf = sb("bf", [P, D], F32)
        wqk1 = sb("wqk1", [P, DC, 2 * D], F32)
        wv1 = sb("wv1", [P, DC, D], F32)
        wo1 = sb("wo1", [P, DC, D], F32)
        wr = sb("wr", [P, DC, D], F32)
        wk = sb("wk", [P, DC, D], F32)
        wv = sb("wv", [P, DC, D], F32)
        mu = sb("mu", [P, 2, DC], F32)
        omu = sb("omu", [P, 2, DC], F32)
        tmp = sb("tmp", [P, 4, 2 * D], F32)
        tmp16 = sb("tmp16", [P, 4, 2 * D], F16)
        stack = sb("stack", [P, 2, 2, HG * T], BF16)
        v1 = sb("v1", [P, NT, H, VW], F32)
        probs = sb("probs", [P, 2 * HG, CH], F32)
        mx0 = sb("mx0", [P, NT, NQ], F32)
        nmax0 = sb("nmax0", [P, NT], F32)
        nmaxT0 = sb("nmaxT0", [TPC, P], F32)
        mx1 = sb("mx1", [P, HG, NT, NQ], F32)
        nmax1 = sb("nmax1", [P, HG * TPC], F32)
        nmaxb = sb("nmaxb", [P, HG, MAXROWS, TPC], BF16)
        nmaxT1 = sb("nmaxT1", [HG * MAXROWS * TPC, 2, P], BF16)
        junk = sb("junk", [P, 4, CH], BF16)
        osb = sb("osb", [P, 2, CH], F32)
        rec = sb("rec", [P, TPC, HG], F32)

        def words(i, side):
            return stack[:, i, side, :].bitcast(F32)

        def tiles(ap, width):
            return ap.rearrange("p (t v) -> p t v", v=width)

        qa = words(0, 0)[0:DK0 + 2, 0:T]
        ka = words(0, 0)[0:DK0 + 2, T:2 * T]
        ctxT = words(0, 1)[0:DK0 + 1, 0:T]
        v0 = tiles(words(1, 0)[:, 0:NT * (DK0 + 1)], DK0 + 1)
        ctx0 = tiles(words(1, 0)[:, T:T + NT * (DK0 + 1)], DK0 + 1)
        xr = words(0, 0).rearrange("p (c t) -> p c t", c=DC)
        xk = words(0, 1).rearrange("p (c t) -> p c t", c=DC)
        gate = tiles(words(1, 0), D)
        kact = words(1, 1).rearrange("p (c t) -> p c t", c=DC)
        qs = [stack[:, i, 0, :].rearrange("p (h t) -> p h t", h=HG) for i in range(2)]
        ks = [stack[:, i, 1, :].rearrange("p (h t) -> p h t", h=HG) for i in range(2)]
        att = xn
        xnf = xn[:, :, :].rearrange("p t d -> p (t d)")
        qcos, qsin, qkc = [[xnf[:, (2 * k + i) * CH:(2 * k + i + 1) * CH] for i in range(2)] for k in range(3)]
        resid = [tmp[:, i, :] for i in range(4)]
        roped = probs
        third = sb("third", [P, PARTS * CH], BF16)
        parts = [ap[:, 0:PARTS * CH].rearrange("p (r n) -> p r n", r=PARTS) for ap in (
            xnf[:, 6 * CH:8 * CH].bitcast(BF16), tmp16[:, :, :].rearrange("p i n -> p (i n)").bitcast(BF16),
            third, osb[:, :, :].rearrange("p i n -> p (i n)").bitcast(BF16))]
        parts_dram = nc.dram_tensor("parts_dram", [2, PARTS, D, T], BF16, kind="Internal").ap()

        s_w0 = sem("s_w0")
        s_w1 = sem("s_w1")
        s_const = sem("s_const")
        s_wq = sem("s_wq")
        s_ready = sem("s_ready")
        s_x = [sem(f"s_x{g}") for g in range(NQ)]
        s_agg = sem("s_agg")
        s_eps = sem("s_eps")
        s_rstd = sem("s_rstd")
        s_shift = sem("s_shift")
        s_norm = sem("s_norm")
        s_last = sem("s_last")
        s_mm = sem("s_mm")
        s_ea = sem("s_ea")
        s_ed = sem("s_ed")
        s_fill = sem("s_fill")
        s_xp = sem("s_xp")
        s_xd = sem("s_xd")
        s_bp = sem("s_bp")
        s_bd = sem("s_bd")
        s_prod = sem("s_prod")
        s_p1 = sem("s_p1")
        s_m1 = sem("s_m1")
        s_nm0 = sem("s_nm0")
        s_row0 = sem("s_row0")
        s_s0 = sem("s_s0")
        s_e0 = sem("s_e0")
        s_v0 = sem("s_v0")
        s_oe = sem("s_oe")
        s_ot = sem("s_ot")
        s_oc = sem("s_oc")
        s_rt = sem("s_rt")
        s_rope = sem("s_rope")
        s_re = sem("s_re")
        s_mid = sem("s_mid")
        s_lo = sem("s_lo")
        s_pd = [sem(f"s_pd{i}") for i in range(4)]
        s_first = [sem(f"s_first{q}") for q in range(NQ)]
        s_stk = [sem(f"s_stk{i}") for i in range(2)]
        s_p2 = sem("s_p2")
        s_m2 = sem("s_m2")
        s_nm1 = sem("s_nm1")
        s_row1 = [sem(f"s_row1{i}") for i in range(2)]
        s_o1 = sem("s_o1")
        s_vp = sem("s_vp")
        s_ve = sem("s_ve")
        s_s1 = sem("s_s1")
        s_e1 = sem("s_e1")
        s_v1 = sem("s_v1")
        s_mix = sem("s_mix")
        s_gate = sem("s_gate")
        s_ku = sem("s_ku")
        s_out = sem("s_out")
        s_link = sem("s_link")
        s_pl = sem("s_pl")
        s_apart = sem("s_apart")

        XJOBS = 4 * 4
        PJOBS = 4 * NQ
        OUTS = NHG * NQ
        ROWS = 16 * HG
        STK = 16 * 2 * len(TERMS)
        STKS = [len(range(i, NHG, 2)) - (i == 0) for i in range(2)]
        FILLS = 7
        LINKS = 4 * NQ + 2 * NQ + PJOBS // 2 + 2 * OUTS + OUTS
        PLINKS = 4
        NCONST = 9
        W0, W1 = 16 * 10, 16 * 7

        def apart(eng):
            eng.sem_inc(s_apart, 1)

        def normalised(eng, b, ln, g):
            if g == NQ - 1:
                eng.wait_ge(s_last, b * 4 + ln + 1)
            else:
                eng.wait_ge(s_norm, b * 4 * (NQ - 1) + ln * (NQ - 1) + g + 1)

        def parts_out(eng, b):
            for i in range(4):
                eng.wait_ge(s_pd[i], b * 4 * PJOBS + 4 * PJOBS)

        block = ctx.enter_context(nc.Block())

        @block.sync
        def _(sp):
            def cw(a):
                return a.rearrange("(c p) n -> p c n", p=P)

            for dst, src in [
                (wqk0[:, :, :], cw(w["wqk0"])),
                (wv0[:, :, :], cw(w["wv0"])),
                (wo0[0:DK0, :], w["wo0"]),
                (wo0[DK0:DK0 + 1, :], w["bo0"].rearrange("(a d) -> a d", a=1)),
                (bqk0[:, :], w["bqk0"]),
                (bv0[:, :], w["bv0"].rearrange("(a d) -> a d", a=1).broadcast_to([P, DK0])),
                (tmp[:, 0, :].rearrange("p (c d) -> p c d", c=DC), cw(w["wf"])),
                (bf[:, :], w["bf"].rearrange("(a d) -> a d", a=1).broadcast_to([P, D])),
                (cos[:, :, :], w["cos"].rearrange("(t p) d -> p t d", p=P)),
                (sin[:, :, :], w["sin"].rearrange("(t p) d -> p t d", p=P)),
            ]:
                sp.dma_start(dst, src).then_inc(s_w0, 16)

            with sp.Fori(0, B) as b:
                for g in range(NQ):
                    sp.dma_start(x[:, TPC * g:TPC * (g + 1), :],
                                 x_in[bass.ds(b, 1), CH * g:CH * (g + 1), :]
                                 .rearrange("o (t p) d -> p (o t) d", p=P)).then_inc(s_x[g], 16)
                for q in range(NQ):
                    sp.wait_ge(s_m1, b * UNITS0 + MAX0.index((None, q)) + 1)
                    sp.dma_start(qa[DK0 + 1:DK0 + 2, CH * q:CH * (q + 1)], nmaxT0[:, :]).then_inc(s_row0, 16)
                def load_stack(hg, cols, loaded):
                    for side in range(2):
                        to = (qs, ks)[side][hg % 2]
                        for n, term in enumerate(TERMS):
                            rows = parts_dram[side, term[side], HG * DK1 * hg:HG * DK1 * (hg + 1), cols]
                            sp.dma_start(to[DK1 * n:DK1 * (n + 1), :, cols],
                                         rows.rearrange("(h d) t -> d h t", h=HG)).then_inc(loaded, 16)

                for n in range(PJOBS):
                    g, bl = divmod(n, 4)
                    sp.wait_ge(s_lo, b * PJOBS + n + 1)
                    sp.dma_start(
                        parts_dram[bl // 2, :, (bl % 2) * P:(bl % 2 + 1) * P, CH * g:CH * (g + 1)]
                        .rearrange("r p n -> p r n"), parts[n % 4][:, :, :]).then_inc(s_pd[n % 4], 16)

                    if bl == 3:
                        sp.wait_ge(s_pd[0], b * 4 * PJOBS + 16 * (g + 1))
                        apart(sp)
                        sp.wait_ge(s_pd[2], b * 4 * PJOBS + 16 * (g + 1))
                        apart(sp)
                        load_stack(0, slice(CH * g, CH * (g + 1)), s_first[g])
                parts_out(sp, b)
                load_stack(1, slice(0, T), s_stk[1])
                for kind, item in PLAN1:
                    if kind == "turned max":
                        hg, q = item
                        oq = NQ * hg + q
                        sp.wait_ge(s_m2, b * UNITS1 + UNIT1[kind, item] + 1)
                        for h in range(HG):
                            sp.dma_start(qs[hg % 2][KS:KS + MAXROWS, h, CH * q:CH * (q + 1)],
                                         nmaxT1[MAXROWS * TPC * h:MAXROWS * TPC * (h + 1), oq % 2, :]
                                         ).then_inc(s_row1[oq % 2], 16)
                    elif kind == "scores" and item[1] == SUBS - 1 and item[0] + 2 < NHG:
                        sp.wait_ge(s_s1, b * NHG * SUBS + SUBS * (item[0] + 1))
                        load_stack(item[0] + 2, slice(0, T), s_stk[item[0] % 2])
                for g in range(NQ):
                    sp.wait_ge(s_xp, b * XJOBS + XJOBS - NQ + g + 1)
                    apart(sp)
                    sp.wait_ge(s_xd, b * 8 + 4 + g + 1)
                    apart(sp)
                    sp.dma_start(y_out[bass.ds(b, 1), CH * g:CH * (g + 1), :]
                                 .rearrange("o (t p) d -> p (o t) d", p=P),
                                 x[:, TPC * g:TPC * (g + 1), :]).then_inc(s_out, 16)
                sp.wait_ge(s_out, b * 16 * NQ + 16 * NQ)
                apart(sp)

        @block.gpsimd
        def _(pool):
            pool.memset(ident[:, :], 0.0).then_inc(s_const, 1)
            pool.memset(maskq[:, :], 0.0).then_inc(s_const, 1)
            pool.memset(maskk[:, :], 0.0).then_inc(s_const, 1)
            pool.memset(mhalf[:, :], -0.5).then_inc(s_const, 1)
            pool.memset(xnT[:, :, 0:1], 0.0).then_inc(s_const, 1)
            pool.wait_ge(s_const, 5)
            pool.affine_select(out=ident[:, :], in_=ident[:, :], compare_op=ALU.not_equal, fill=1.0,
                               base=0, pattern=[[-1, P]], channel_multiplier=1).then_inc(s_const, 1)
            pool.affine_select(out=maskq[:, CH - P:CH], in_=maskq[:, CH - P:CH], compare_op=ALU.is_ge, fill=NEG,
                               base=0, pattern=[[-1, P]], channel_multiplier=1).then_inc(s_const, 1)
            pool.affine_select(out=maskk[:, :], in_=maskk[:, :], compare_op=ALU.is_ge, fill=NEG,
                               base=0, pattern=[[1, P]], channel_multiplier=-1).then_inc(s_const, 1)
            pool.wait_ge(s_const, 8)
            pool.tensor_copy(identb[:, :], ident[:, :]).then_inc(s_const, 1)

            with pool.Fori(0, B) as b:
                plinks = [0]

                def plink(ins):
                    plinks[0] += 1
                    ins.then_inc(s_pl, 1)
                    pool.wait_ge(s_pl, b * PLINKS + plinks[0])

                def roots(ln, g):
                    ts = slice(TPC * g, TPC * (g + 1))
                    count = b * 4 * NQ + ln * NQ + g + 1
                    pool.wait_ge(s_agg, count)
                    apart(pool)
                    pool.tensor_scalar(vare[:, ts], mv[:, ts, 1], EPS, None, ALU.add)
                    pool.tensor_scalar(shift[:, ts], mv[:, ts, 0], -1.0, None, ALU.mult).then_inc(s_eps, 1)
                    pool.wait_ge(s_eps, count)
                    pool.tensor_tensor(rstd[:, ts], vare[:, ts], mhalf[:, ts], ALU.pow).then_inc(s_rstd, 1)
                    pool.wait_ge(s_rstd, count)
                    pool.tensor_tensor(shift[:, ts], shift[:, ts], rstd[:, ts], ALU.mult).then_inc(s_shift, 1)

                def read_by_act(stage, e):
                    pool.wait_ge(s_ea, b * EJOBS + FIRST[stage] // 2 + e + 1)

                def adds_and_roots(stage, ln):
                    source = tmp16 if stage == "FFN" else tmp
                    for e in range(4):
                        xs = x[:, 4 * e:4 * e + 2, :].rearrange("p t d -> p (t d)")
                        read_by_act(stage, e)
                        pool.tensor_tensor(xs, source[:, e % 2, :], xs, ALU.add).then_inc(s_xp, 1)
                        if e >= 2:
                            roots(ln, e - 2)
                    roots(ln, 2)
                    roots(ln, 3)

                for g in range(NQ):
                    roots(0, g)
                pool.wait_ge(s_shift, b * 4 * NQ + NQ)
                fills = [(qa[DK0:DK0 + 2, :], 0.0), (ka[DK0:DK0 + 2, :], 1.0),
                         (v0[:, :, DK0:DK0 + 1], 1.0), (ctx0[:, :, DK0:DK0 + 1], 1.0),
                         (stack[KS:P, 0, 1, :], 1.0), (stack[KS:P, 1, 1, :], 1.0), (v1[:, :, :, DK1:VW], 1.0)]
                for n, (rows, value) in enumerate(fills):
                    if n > 0:
                        pool.wait_ge(s_fill, b * FILLS + n)
                    apart(pool)
                    pool.memset(rows, value).then_inc(s_fill, 1)
                pool.wait_ge(s_fill, b * FILLS + len(fills))
                adds_and_roots("WO0", 1)
                for e in range(4):
                    xs = x[:, 4 * e:4 * e + 2, :]
                    normalised(pool, b, 1, e)
                    pool.tensor_tensor(xs, xs, bf[:, :].unsqueeze(1).broadcast_to([P, 2, D]),
                                       ALU.add).then_inc(s_bp, 1)
                pool.wait_ge(s_bp, b * 4 + 4)
                adds_and_roots("FFN", 2)
                for k, (key, g) in enumerate(QKR):
                    for i in range(TPC):
                        if key == "QK":
                            t = TPC * g + i
                            if i % 2 == 0:
                                pool.wait_ge(s_rt, b * (NT // 2) + t // 2 + 1)
                            else:
                                pool.wait_ge(s_ed, b * EJOBS + (FIRST["QKR"] + TPC * k + i) // 2 + 1)
                            pool.tensor_tensor(roped[:, t % 8, :], qcos[t % 2], qsin[t % 2],
                                               ALU.add).then_inc(s_rope, 1)
                        else:
                            n = 4 * g + i
                            pool.wait_ge(s_mid, b * PJOBS + n + 1)
                            pool.tensor_tensor(parts[n % 4][:, 2, :], resid[n % 4], parts[n % 4][:, 1, :],
                                               ALU.subtract).then_inc(s_lo, 1)
                adds_and_roots("WO1", 3)
                for n in range(8):
                    q, c = divmod(n, DC)
                    if n % 2 == 0:
                        read_by_act("K", n // 2)
                    else:
                        pool.wait_ge(s_ed, b * EJOBS + FIRST["K"] // 2 + n // 2 + 1)
                    u = tmp[:, (n % 2) * 2 + n // 2 % 2, :]
                    pool.tensor_tensor(kact[:, c, CH * q:CH * (q + 1)], u, u, ALU.mult).then_inc(s_ku, 1)
                for e in range(4):
                    xs = x[:, 4 * e:4 * e + 2, :].rearrange("p t d -> p (t d)")
                    gs = gate[:, 4 * e:4 * e + 2, :].rearrange("p t d -> p (t d)")
                    read_by_act("V", e)
                    plink(pool.tensor_tensor(tmp[:, e % 2, :], tmp[:, e % 2, :], gs, ALU.mult))
                    pool.tensor_tensor(xs, xs, tmp[:, e % 2, :], ALU.add).then_inc(s_xp, 1)
                assert plinks[0] == PLINKS

        @block.scalar
        def _(act):
            def cw(a):
                return a.rearrange("(c p) n -> p c n", p=P)

            for dst, src in [
                (wqk1[:, :, :], cw(w["wqk1"])), (wv1[:, :, :], cw(w["wv1"])), (wo1[:, :, :], cw(w["wo1"])),
                (wr[:, :, :], cw(w["wr"])), (wk[:, :, :], cw(w["wk"])), (wv[:, :, :], cw(w["wv"])),
                (mu[:, :, :], w["mu"]),
            ]:
                act.dma_start(dst, src).then_inc(s_w1, 16)
            act.wait_ge(s_w0, W0)

            with act.Fori(0, B) as b:
                def job(stage, e):
                    j = FIRST[stage] + 2 * e
                    act.wait_ge(s_mm, b * JOBS + j + 1)
                    return bank(j // 2 % 4)

                def scale(ln, g):
                    act.wait_ge(s_shift, b * 4 * NQ + ln * NQ + g + 1)
                    for t in range(TPC * g, TPC * (g + 1)):
                        last = act.activation(xn[:, t, :], x[:, t, :], ACT.Identity, bias=shift[:, t:t + 1],
                                              scale=rstd[:, t:t + 1])
                    last.then_inc(s_norm, 1)

                def turned(stage, ln=None, dst=xnT, after=None):
                    if ln is not None:
                        scale(ln, 0)
                    for g in range(NQ):
                        if ln is not None and g + 1 < NQ - 1:
                            scale(ln, g + 1)
                        ps = job(stage, g)
                        apart(act)
                        if dst is xqT:
                            ins = act.activation(dst[:, 0, CH * g:CH * (g + 1)], ps, ACT.Copy, saturate=False)
                        else:
                            ins = act.activation(dst[:, 0, 1 + CH * g:1 + CH * (g + 1)], ps, ACT.Copy)
                        ins.then_inc(s_ea, 1)
                        if after and g >= 1:
                            after(g - 1)
                    if after:
                        after(NQ - 1)

                def products(g):
                    act.wait_ge(s_ea, b * EJOBS + FIRST["T3"] // 2 + g + 1)
                    act.wait_ge(s_ed, b * EJOBS + FIRST["T3"] // 2 + g + 1)
                    ts = slice(CH * g, CH * (g + 1))
                    for i, to in enumerate((xr, xk)):
                        for c in range(DC):
                            last = act.activation(to[:, c, ts], xnT[:, c, ts], ACT.Identity,
                                                  scale=omu[:, i, c:c + 1])
                    last.then_inc(s_prod, 1)

                def to_pool(stage, dst, func, used, per_batch, count):
                    for e in range(4):
                        ps = job(stage, e)
                        if e >= 2:
                            act.wait_ge(used, b * per_batch + count(e - 2))
                        elif stage == "V":
                            act.wait_ge(s_ku, b * 8 + 2 * e + 5)
                        act.activation(dst[:, e % 2, :], ps, func).then_inc(s_ea, 1)

                turned("T0", 0)
                for q in range(NQ):
                    ps = job("QK0", q)
                    act.activation(qa[0:DK0, CH * q:CH * (q + 1)], ps[0:DK0, :], ACT.Identity,
                                   bias=bqk0[:, 0:1]).then_inc(s_ea, 1)
                ps = job("V0", 0)
                act.activation(v0[:, 0:NT // 2, 0:DK0], tiles(ps, DK0), ACT.Copy).then_inc(s_ea, 1)
                for k, (q, kb) in enumerate(ORDER):
                    off = span(q, kb)
                    if k >= 4:
                        act.wait_ge(s_v0, b * STEPS + k - 3)
                    act.wait_ge(s_s0, b * STEPS + k + 1)
                    act.activation(probs[:, k % 4, 0:CH - off], bank(k % 4, 0, CH - off), ACT.Exp,
                                   scale=DK0 ** -0.5).then_inc(s_e0, 1)
                for e in range(2):
                    ps = job("CT0", e)
                    act.activation(ctxT[:, 2 * CH * e:2 * CH * e + CH], ps[0:DK0 + 1, :],
                                   ACT.Copy).then_inc(s_ea, 1)
                to_pool("WO0", tmp, ACT.Copy, s_xp, XJOBS, lambda e: e + 1)
                turned("T1", 1, xqT)
                to_pool("FFN", tmp16, ACT.Copy, s_xp, XJOBS, lambda e: 4 + e + 1)
                turned("T2", 2)
                for n, (key, g) in enumerate(QKR):
                    for i in range(0, TPC, 2):
                        ps = job("QKR", (TPC * n + i) // 2)
                        if key == "QK":
                            t = TPC * g + i
                            if t >= 4:
                                act.wait_ge(s_rt, b * (NT // 2) + t // 2 - 1)
                            act.activation(qkc[t // 2 % 2], ps, ACT.Copy).then_inc(s_ea, 1)
                        else:
                            m = 4 * g + i
                            if m >= 4:
                                act.wait_ge(s_pd[m % 4], b * 4 * PJOBS + 16 * (m // 4))
                            act.activation(resid[m % 4], ps, ACT.Copy)
                            act.activation(parts[m % 4][:, 0, :], ps, ACT.Copy).then_inc(s_ea, 1)
                    if key == "RT":
                        for i in range(TPC):
                            m = 4 * g + i
                            if i % 2 == 0:
                                act.wait_ge(s_re, b * (PJOBS // 2) + m // 2 + 1)
                            else:
                                act.wait_ge(s_ed, b * EJOBS + (FIRST["QKR"] + TPC * n + i) // 2 + 1)
                            act.activation(parts[m % 4][:, 1, :], resid[m % 4], ACT.Copy).then_inc(s_mid, 1)
                for kind, item in PLAN1:
                    if kind == "project":
                        t = item[1]
                        act.wait_ge(s_vp, b * NT + t + 1)
                        act.activation(v1[:, t, :, 0:DK1], tiles(bank(t % 4, 0, D), DK1), ACT.Copy).then_inc(s_ve, 1)
                        if t == NT - 1:
                            parts_out(act, b)
                    elif kind == "scores":
                        hg, s = item
                        k, pair = divmod(s, 2)
                        off = span(*ORDER[k])
                        at = SUBS * hg + s
                        if at >= 4:
                            act.wait_ge(s_v1, b * NHG * STEPS + at // 2 - 1)
                        act.wait_ge(s_s1, b * NHG * SUBS + at + 1)
                        two = psum[:, 2 * pair * CH:2 * (pair + 1) * CH].rearrange("p (h n) -> p h n", h=2)
                        at = HG * (k % 2) + 2 * pair
                        act.activation(probs[:, at:at + 2, 0:CH - off], two[:, :, 0:CH - off], ACT.Exp,
                                       scale=DK1 ** -0.5).then_inc(s_e1, 1)
                    elif kind == "copy out":
                        hg, q = item
                        oq = NQ * hg + q
                        if oq >= 2:
                            before = ("turned out", divmod(oq - 2, NQ))
                            act.wait_ge(s_p2, b * UNITS1 + UNIT1[before] + 1)
                        k = ORDER.index((q, TPC * (q + 1) - 1))
                        act.wait_ge(s_v1, b * NHG * STEPS + STEPS * hg + k + 1)
                        act.activation(osb[:, oq % 2, :], bank(7), ACT.Copy).then_inc(s_o1, 1)
                turned("AT1")
                to_pool("WO1", tmp, ACT.Copy, s_xp, XJOBS, lambda e: 8 + e + 1)
                turned("T3", 3, after=products)
                for e in range(4):
                    ps = job("R", e)
                    act.activation(gate[:, 4 * e:4 * e + 2, :], tiles(ps, D), ACT.Sigmoid).then_inc(s_ea, 1)
                    act.wait_ge(s_ed, b * EJOBS + FIRST["R"] // 2 + e + 1)
                    act.activation(gate[:, 4 * e + 2:4 * e + 4, :], gate[:, 4 * e + 2:4 * e + 4, :],
                                   ACT.Sigmoid).then_inc(s_gate, 1)
                to_pool("K", tmp, ACT.Relu, s_ku, 8, lambda e: 2 * e + 1)
                to_pool("V", tmp, ACT.Copy, s_xp, XJOBS, lambda e: 12 + e + 1)

        @block.vector
        def _(dve):
            chain = [0]

            def then(ins):
                chain[0] += 1
                ins.then_inc(s_wq, 1)
                dve.wait_ge(s_wq, chain[0])

            raw, small, large, pick = (tmp[:, i, :] for i in range(4))
            dve.wait_ge(s_w0, W0)
            dve.tensor_tensor(pick, raw, raw, ALU.mult)
            dve.tensor_scalar(small, raw, 128.0, -128.0, ALU.min, ALU.max)
            then(dve.tensor_scalar(large, raw, 448.0, -448.0, ALU.min, ALU.max))
            dve.tensor_scalar(pick, pick, 128.0 ** 2, None, ALU.is_gt)
            dve.tensor_copy(wf8[:, 0, :], small, saturate=False)
            then(dve.tensor_scalar(wf8[:, 1, :], large, 0.5, None, ALU.mult, saturate=False))
            dve.tensor_copy(small, wf8[:, 0, :])
            then(dve.tensor_scalar(large, wf8[:, 1, :], 2.0, None, ALU.mult))
            then(dve.tensor_tensor(large, large, small, ALU.subtract))
            then(dve.tensor_tensor(large, large, pick, ALU.mult))
            dve.tensor_tensor(wf[:, :, :].rearrange("p c d -> p (c d)"), small, large, ALU.add)
            dve.memset(psum[:, :], 0.0)
            dve.wait_ge(s_w1, W1)
            dve.tensor_scalar(omu[:, :, :], mu[:, :, :], -1.0, 1.0, ALU.mult, ALU.add).then_inc(s_ready, 1)
            dve.wait_ge(s_const, NCONST)

            with dve.Fori(0, B) as b:
                links = [0]

                def link(ins):
                    links[0] += 1
                    ins.then_inc(s_link, 1)
                    dve.wait_ge(s_link, b * LINKS + links[0])

                def statistics(ln, g):
                    if ln == 0:
                        dve.wait_ge(s_x[g], b * 16 + 16)
                    else:
                        dve.wait_ge(s_xp, b * XJOBS + 4 * (ln - 1) + g + 1)
                        if ln == 2:
                            dve.wait_ge(s_xd, b * 8 + g + 1)
                        else:
                            stage = {1: "WO0", 3: "WO1"}[ln]
                            dve.wait_ge(s_ed, b * EJOBS + FIRST[stage] // 2 + g + 1)
                    for t in range(TPC * g, TPC * (g + 1)):
                        last = dve.bn_stats(stats[:, t, :], x[:, t, :])
                    link(last)
                    apart(dve)
                    for t in range(TPC * g, TPC * (g + 1)):
                        last = dve.bn_aggr(mv[:, t, :], stats[:, t, :])
                    last.then_inc(s_agg, 1)

                def scale_last(ln):
                    dve.wait_ge(s_shift, b * 4 * NQ + ln * NQ + NQ)
                    for t in range(NT - TPC, NT):
                        last = dve.tensor_scalar(xn[:, t, :], x[:, t, :], mv[:, t, 0:1], rstd[:, t:t + 1],
                                                 ALU.subtract, ALU.mult)
                    last.then_inc(s_last, 1)

                def job(stage, e):
                    j = FIRST[stage] + 2 * e + 1
                    dve.wait_ge(s_mm, b * JOBS + j + 1)
                    return bank(4 + j // 2 % 4)

                def turned(stage, dst=xnT, after=None):
                    for g in range(NQ):
                        ps = job(stage, g)
                        apart(dve)
                        col = 0 if dst is xqT else 1
                        kind = {"saturate": False} if dst is xqT else {}
                        dve.tensor_copy(dst[:, 1, col + CH * g:col + CH * (g + 1)], ps, **kind).then_inc(s_ed, 1)
                        if after and g >= 1:
                            after(g - 1)
                    if after:
                        after(NQ - 1)

                def adds_and_statistics(stage, ln):
                    for e in range(4):
                        ps = job(stage, e)
                        xs = x[:, 4 * e + 2:4 * e + 4, :]
                        if stage == "FFN":
                            t16 = tiles(tmp16[:, 2 + e % 2, :], D)
                            dve.tensor_copy(t16, tiles(ps, D)).then_inc(s_ed, 1)
                            dve.wait_ge(s_bd, b * 4 + e + 1)
                            dve.wait_ge(s_ed, b * EJOBS + FIRST["FFN"] // 2 + e + 1)
                            dve.tensor_tensor(xs, t16, xs, ALU.add).then_inc(s_xd, 1)
                        else:
                            dve.tensor_tensor(xs, tiles(ps, D), xs, ALU.add).then_inc(s_ed, 1)
                        if e >= 1:
                            statistics(ln, e - 1)
                    statistics(ln, 3)
                    scale_last(ln)

                def add_bias(e):
                    xs = x[:, 4 * e + 2:4 * e + 4, :]
                    normalised(dve, b, 1, e)
                    dve.tensor_tensor(xs, xs, bf[:, :].unsqueeze(1).broadcast_to([P, 2, D]),
                                      ALU.add).then_inc(s_bd, 1)

                for g in range(NQ):
                    statistics(0, g)
                scale_last(0)
                turned("T0")
                for q in range(NQ):
                    ps = job("QK0", q)
                    dve.tensor_scalar(ka[0:DK0, CH * q:CH * (q + 1)], ps[0:DK0, :], bqk0[:, 1:2], None,
                                      ALU.add).then_inc(s_ed, 1)
                ps = job("V0", 0)
                dve.tensor_copy(v0[:, NT // 2:NT, 0:DK0], tiles(ps, DK0)).then_inc(s_ed, 1)

                def read_scores(ps, n, diagonal, out, slot):
                    if diagonal:
                        apart(dve)
                        ins = dve.tensor_tensor_reduce(junk[:, slot, 0:n], ps, maskq[:, CH - n:CH], 1.0, -3e38,
                                                       ALU.add, ALU.max, out)
                    else:
                        ins = dve.tensor_reduce(out, ps, AX.X, ALU.max)
                    return ins

                def copy_out(oq, rows):
                    dve.tensor_copy(osb[0:rows, oq % 2, :], bank(6 + oq % 2, rows=rows)).then_inc(s_oe, 1)

                for kind, n in plan0():
                    if kind == "max":
                        i, c = MAX0[n]
                        ps = bank(4 + n % 2)
                        if i is None:
                            dve.wait_ge(s_m1, b * UNITS0 + n)
                            ts = slice(TPC * c, TPC * (c + 1))
                            dve.tensor_reduce(nmax0[:, ts], mx0[:, ts, 0:c + 1], AX.X, ALU.max,
                                              negate=True).then_inc(s_nm0, 1)
                            dve.wait_ge(s_p1, b * UNITS0 + n + 1)
                            if c >= 1:
                                dve.wait_ge(s_row0, b * 16 * NQ + 16 * c)
                            dve.tensor_copy(nmaxT0[:, :], ps[0:TPC, 0:P]).then_inc(s_m1, 1)
                        else:
                            width = CH if c < i // TPC else (i % TPC + 1) * P
                            if n >= 4:
                                dve.wait_ge(s_m1, b * UNITS0 + n - 3)
                            dve.wait_ge(s_p1, b * UNITS0 + n + 1)
                            read_scores(ps[:, 0:width], width, c == i // TPC, mx0[:, i, c:c + 1],
                                        n % 4).then_inc(s_m1, 1)
                    elif kind == "copy out":
                        dve.wait_ge(s_v0, b * STEPS + ORDER.index((n, TPC * (n + 1) - 1)) + 1)
                        copy_out(n, DK0 + 1)
                    elif kind == "turn":
                        dve.wait_ge(s_ot, b * NQ + n + 1)
                        turned_o = tiles(bank(6 + n % 2), P)
                        ts = slice(TPC * n, TPC * (n + 1))
                        link(dve.reciprocal(rec[:, :, 0], turned_o[:, :, DK0]))
                        link(dve.tensor_tensor(ctx0[:, ts, 0:DK0], turned_o[:, :, 0:DK0],
                                               rec[:, :, 0:1].broadcast_to([P, TPC, DK0]), ALU.mult))
                        dve.tensor_tensor(ctx0[:, ts, 0:DK0], ctx0[:, ts, 0:DK0],
                                          bv0[:, :].unsqueeze(1).broadcast_to([P, TPC, DK0]),
                                          ALU.add).then_inc(s_oc, 1)
                for e in range(2):
                    ps = job("CT0", e)
                    dve.tensor_copy(ctxT[:, CH * (2 * e + 1):CH * (2 * e + 2)], ps[0:DK0 + 1, :]).then_inc(s_ed, 1)
                adds_and_statistics("WO0", 1)
                turned("T1", xqT, after=add_bias)
                adds_and_statistics("FFN", 2)
                turned("T2")
                for n, (key, g) in enumerate(QKR):
                    for i in range(TPC):
                        if key == "QK":
                            t = TPC * g + i
                            if i % 2 == 0:
                                dve.wait_ge(s_ea, b * EJOBS + (FIRST["QKR"] + TPC * n + i) // 2 + 1)
                                src = qkc[t // 2 % 2]
                            else:
                                src = job("QKR", (TPC * n + i) // 2)
                            if t >= 2:
                                dve.wait_ge(s_rope, b * NT + t - 1)
                            src = src.rearrange("p (h d) -> p h d", d=DK1)
                            half = DK1 // 2
                            to_cos = qcos[t % 2].rearrange("p (h d) -> p h d", d=DK1)
                            to_sin = qsin[t % 2].rearrange("p (h d) -> p h d", d=DK1)
                            cs = cos[:, t, :].unsqueeze(1)
                            sn = sin[:, t, :].unsqueeze(1)
                            dve.tensor_tensor(to_cos, src, cs.broadcast_to([P, 2 * H, DK1]), ALU.mult)
                            dve.tensor_tensor(to_sin[:, :, 0:half], src[:, :, half:DK1],
                                              sn[:, :, 0:half].broadcast_to([P, 2 * H, half]), ALU.mult)
                            ins = dve.tensor_tensor(to_sin[:, :, half:DK1], src[:, :, 0:half],
                                                    sn[:, :, half:DK1].broadcast_to([P, 2 * H, half]), ALU.mult)
                            ins.then_inc(s_ed if i % 2 else s_rt, 1)
                        else:
                            m = 4 * g + i
                            if i % 2 == 1:
                                ps = job("QKR", (TPC * n + i) // 2)
                                if m >= 4:
                                    dve.wait_ge(s_pd[m % 4], b * 4 * PJOBS + 16 * (m // 4))
                                link(dve.tensor_copy(parts[m % 4][:, 0, :], ps))
                                dve.tensor_tensor(resid[m % 4], ps, parts[m % 4][:, 0, :],
                                                  ALU.subtract).then_inc(s_ed, 1)
                            else:
                                dve.wait_ge(s_ea, b * EJOBS + (FIRST["QKR"] + TPC * n + i) // 2 + 1)
                                dve.tensor_tensor(resid[m % 4], resid[m % 4], parts[m % 4][:, 0, :],
                                                  ALU.subtract).then_inc(s_re, 1)
                for kind, item in PLAN1:
                    if (kind, item) in UNIT1:
                        at = UNIT1[kind, item]
                        ps = bank(4 + at % MB)
                    if kind == "max":
                        hg, i, c, h = item
                        width = CH if c < i // TPC else (i % TPC + 1) * P
                        if at >= 4:
                            dve.wait_ge(s_m2, b * UNITS1 + at - 3)
                        dve.wait_ge(s_p2, b * UNITS1 + at + 1)
                        read_scores(ps[:, 0:width], width, c == i // TPC,
                                    mx1[:, h, i, c:c + 1], at % 4).then_inc(s_m2, 1)
                    elif kind == "minus max":
                        hg, q = item
                        oq = NQ * hg + q
                        dve.wait_ge(s_m2, b * UNITS1 + at + 1)
                        if oq >= 1:
                            before = ("turned max", divmod(oq - 1, NQ))
                            dve.wait_ge(s_p2, b * UNITS1 + UNIT1[before] + 1)
                        link(dve.tensor_reduce(nmax1[:, :].rearrange("p (h t) -> p h t", h=HG),
                                               mx1[:, :, TPC * q:TPC * (q + 1), 0:q + 1],
                                               AX.X, ALU.max, negate=True))
                        minus = nmax1[:, :].rearrange("p (h t) -> p h t", h=HG)
                        link(dve.tensor_copy(nmaxb[:, :, 0, :], minus))
                        dve.tensor_tensor(nmaxb[:, :, 1, :], minus, nmaxb[:, :, 0, :],
                                          ALU.subtract).then_inc(s_nm1, 1)
                    elif kind == "turned max":
                        oq = NQ * item[0] + item[1]
                        if oq >= 2:
                            dve.wait_ge(s_row1[oq % 2], b * (ROWS * OUTS // 2) + ROWS * (oq // 2))
                        dve.wait_ge(s_p2, b * UNITS1 + at + 1)
                        dve.tensor_copy(nmaxT1[:, oq % 2, :],
                                        ps.bitcast(BF16)[0:HG * MAXROWS * TPC, 0:P]).then_inc(s_m2, 1)
                    elif kind == "turned out":
                        hg, q = item
                        if item == (0, 0):
                            parts_out(dve, b)
                        dve.wait_ge(s_m2, b * UNITS1 + at)
                        dve.wait_ge(s_p2, b * UNITS1 + at + 1)
                        turned_o = ps.rearrange("p (t h v) -> p t h v", t=TPC, h=HG)
                        link(dve.reciprocal(rec[:, :, :], turned_o[:, :, :, DK1]))
                        cols = att[:, TPC * q:TPC * (q + 1), HG * DK1 * hg:HG * DK1 * (hg + 1)]
                        dve.tensor_tensor(cols.rearrange("p t (h v) -> p t h v", h=HG),
                                          turned_o[:, :, :, 0:DK1],
                                          rec[:, :, :].unsqueeze(3).broadcast_to([P, TPC, HG, DK1]),
                                          ALU.mult).then_inc(s_m2, 1)

                turned("AT1")
                adds_and_statistics("WO1", 3)

                def mix(g):
                    dve.wait_ge(s_prod, b * NQ + g + 1)
                    ts = slice(CH * g, CH * (g + 1))
                    for i, to in enumerate((xr, xk)):
                        for c in range(DC):
                            last = dve.scalar_tensor_tensor(out=to[:, c, ts], in0=xnT[:, c, 1 + CH * g:1 + CH * (g + 1)],
                                                            scalar=mu[:, i, c:c + 1], in1=to[:, c, ts],
                                                            op0=ALU.mult, op1=ALU.add)
                    last.then_inc(s_mix, 1)

                turned("T3", after=mix)
                for e in range(4):
                    ps = job("R", e)
                    dve.tensor_copy(gate[:, 4 * e + 2:4 * e + 4, :], tiles(ps, D)).then_inc(s_ed, 1)
                for e in range(4):
                    ps = job("K", e)
                    if e >= 2:
                        dve.wait_ge(s_ku, b * 8 + 2 * e - 2)
                    dve.tensor_scalar(tmp[:, 2 + e % 2, :], ps, 0.0, None, ALU.max).then_inc(s_ed, 1)
                for e in range(4):
                    ps = job("V", e)
                    dve.wait_ge(s_gate, b * 4 + e + 1)
                    if e < 2:
                        dve.wait_ge(s_ku, b * 8 + 2 * e + 6)
                    xs = x[:, 4 * e + 2:4 * e + 4, :]
                    t32 = tiles(tmp[:, 2 + e % 2, :], D)
                    dve.tensor_tensor(t32, tiles(ps, D), gate[:, 4 * e + 2:4 * e + 4, :], ALU.mult).then_inc(s_ed, 1)
                    dve.wait_ge(s_ed, b * EJOBS + FIRST["V"] // 2 + e + 1)
                    dve.tensor_tensor(xs, xs, t32, ALU.add).then_inc(s_xd, 1)
                assert links[0] == LINKS, (links[0], LINKS)

        @block.tensor
        def _(pe):
            pe.wait_ge(s_w0, W0)
            pe.wait_ge(s_const, NCONST)
            pe.wait_ge(s_ready, 1)

            with pe.Fori(0, B) as b:
                def job(stage, n):
                    j = FIRST[stage] + n
                    e = j // 2
                    if e >= 4:
                        pe.wait_ge(s_ed if j % 2 else s_ea, b * EJOBS + e - 3)
                    return bank((4 if j % 2 else 0) + e % 4)

                def jobs_read(stage):
                    pe.wait_ge(s_ea, b * EJOBS + FIRST[stage] // 2)
                    pe.wait_ge(s_ed, b * EJOBS + FIRST[stage] // 2)

                def turn(stage, src, ready):
                    for g in range(NQ):
                        ready(g)
                        for c in range(DC):
                            ps = job(stage, 2 * g + c)
                            for i in range(TPC):
                                last = pe.transpose(ps[:, i * P:(i + 1) * P],
                                                    src[:, TPC * g + i, c * P:(c + 1) * P], ident[:, :])
                            last.then_inc(s_mm, 1)

                def turned(stage, g):
                    pe.wait_ge(s_ea, b * EJOBS + FIRST[stage] // 2 + g + 1)
                    pe.wait_ge(s_ed, b * EJOBS + FIRST[stage] // 2 + g + 1)

                def by_tiles(stage, lhs, rhs, ready, chunks=DC):
                    for n in range(NT // 2):
                        if n % 2 == 0:
                            ready(n // 2)
                        ps = job(stage, n)
                        if stage == "FFN":
                            apart(pe)
                        for i in range(2):
                            for c in range(chunks):
                                last = pe.matmul(ps[:, i * D:(i + 1) * D], lhs(c, 2 * n + i), rhs(c),
                                                 start=(c == 0), stop=(c == chunks - 1))
                        last.then_inc(s_mm, 1)

                def tok(c, t):
                    return xnT[:, c, 1 + P * t:1 + P * (t + 1)]

                turn("T0", xn, lambda g: normalised(pe, b, 0, g))
                for n in range(2 * NQ):
                    q, side = divmod(n, 2)
                    if side == 0:
                        turned("T0", q)
                    ps = job("QK0", n)
                    for c in range(DC):
                        last = pe.matmul(ps[0:DK0, :], wqk0[:, c, side * DK0:(side + 1) * DK0],
                                         xnT[:, c, 1 + CH * q:1 + CH * (q + 1)], start=(c == 0), stop=(c == DC - 1))
                    last.then_inc(s_mm, 1)
                for n in range(2):
                    ps = job("V0", n)
                    for i in range(NT // 2):
                        for c in range(DC):
                            last = pe.matmul(ps[:, i * DK0:(i + 1) * DK0], tok(c, NT // 2 * n + i), wv0[:, c, :],
                                             start=(c == 0), stop=(c == DC - 1))
                    last.then_inc(s_mm, 1)

                jobs_read("CT0")
                pe.wait_ge(s_fill, b * FILLS + 4)
                for kind, n in plan0():
                    if kind == "max":
                        i, c = MAX0[n]
                        if n >= 2:
                            pe.wait_ge(s_m1, b * UNITS0 + n - 1)
                        ps = bank(4 + n % 2)
                        if i is None:
                            pe.wait_ge(s_nm0, b * NQ + c + 1)
                            pe.transpose(ps[0:TPC, 0:P], nmax0[:, TPC * c:TPC * (c + 1)], ident[:, :]).then_inc(s_p1, 1)
                        else:
                            width = CH if c < i // TPC else (i % TPC + 1) * P
                            pe.matmul(ps[:, 0:width], qa[0:DK0 + 1, P * i:P * (i + 1)],
                                      ka[0:DK0 + 1, CH * c:CH * c + width], start=True, stop=True).then_inc(s_p1, 1)
                    elif kind == "scores":
                        q, kb = ORDER[n]
                        off = span(q, kb)
                        if kb == 0:
                            pe.wait_ge(s_row0, b * 16 * NQ + 16 * (q + 1))
                        if n >= 4:
                            pe.wait_ge(s_e0, b * STEPS + n - 3)
                        diagonal = kb >= TPC * q
                        ins = pe.matmul(bank(n % 4, 0, CH - off), ka[0:DK0 + 2, P * kb:P * (kb + 1)],
                                        qa[0:DK0 + 2, CH * q + off:CH * (q + 1)], start=True, stop=not diagonal)
                        if diagonal:
                            ins = pe.matmul(bank(n % 4, 0, P), identb[:, :], maskk[:, :], start=False, stop=True)
                        ins.then_inc(s_s0, 1)
                    elif kind == "values":
                        q, kb = ORDER[n]
                        off = span(q, kb)
                        if kb == 0 and q >= 2:
                            pe.wait_ge(s_oc, b * NQ + q - 1)
                        pe.wait_ge(s_e0, b * STEPS + n + 1)
                        pe.matmul(bank(6 + q % 2, off, CH, rows=DK0 + 1), v0[:, kb, :], probs[:, n % 4, 0:CH - off],
                                  start=(kb == 0), stop=last_block(n)).then_inc(s_v0, 1)
                    elif kind == "turn":
                        pe.wait_ge(s_oe, b * NQ + n + 1)
                        for i in range(TPC):
                            ins = pe.transpose(bank(6 + n % 2, P * i, P * i + DK0 + 1),
                                               osb[0:DK0 + 1, n % 2, P * i:P * (i + 1)],
                                               ident[0:DK0 + 1, 0:DK0 + 1])
                        ins.then_inc(s_ot, 1)
                pe.wait_ge(s_oc, b * NQ + NQ)
                for n in range(NQ):
                    ps = job("CT0", n)
                    apart(pe)
                    for i in range(TPC):
                        last = pe.transpose(ps[0:DK0 + 1, P * i:P * (i + 1)], ctx0[:, TPC * n + i, :], ident[:, :])
                    last.then_inc(s_mm, 1)

                def context(g):
                    pe.wait_ge(s_ed if g % 2 else s_ea, b * EJOBS + FIRST["CT0"] // 2 + g // 2 + 1)

                by_tiles("WO0", lambda c, t: ctxT[:, P * t:P * (t + 1)], lambda c: wo0[:, :], context, 1)

                turn("T1", xn, lambda g: normalised(pe, b, 1, g))
                by_tiles("FFN", lambda c, t: xqT[:, c, P * t:P * (t + 1)], lambda c: wf[:, c, :],
                         lambda g: turned("T1", g))

                turn("T2", xn, lambda g: normalised(pe, b, 2, g))
                for n, (key, g) in enumerate(QKR):
                    if key == "QK":
                        turned("T2", g)
                    else:
                        pe.wait_ge(s_rope, b * NT + TPC * (g + 1))
                    for i in range(TPC):
                        ps = job("QKR", TPC * n + i)
                        if key == "QK":
                            for c in range(DC):
                                last = pe.matmul(ps, tok(c, TPC * g + i), wqk1[:, c, :],
                                                 start=(c == 0), stop=(c == DC - 1))
                        else:
                            for t in range(TPC):
                                last = pe.transpose(ps[:, P * t:P * (t + 1)],
                                                    roped[:, (TPC * g + t) % 8, P * i:P * (i + 1)], ident[:, :])
                        last.then_inc(s_mm, 1)

                pe.wait_ge(s_ea, b * EJOBS + FIRST["AT1"] // 2)
                pe.wait_ge(s_fill, b * FILLS + FILLS)
                for kind, item in PLAN1:
                    if (kind, item) == ("max", (0, 0, 0, 0)):
                        pe.wait_ge(s_ed, b * EJOBS + FIRST["AT1"] // 2)
                    if (kind, item) in UNIT1:
                        at = UNIT1[kind, item]
                        if at >= MB:
                            pe.wait_ge(s_m2, b * UNITS1 + at - MB + 1)
                        ps = bank(4 + at % MB)
                    if kind == "max":
                        hg, i, c, h = item
                        if hg == 0 and (i % TPC, c, h) == (0, 0, 0):
                            pe.wait_ge(s_first[i // TPC], b * STK + STK)
                        elif hg > 0 and (i, c, h) == (0, 0, 0):
                            pe.wait_ge(s_stk[hg % 2], b * (STK * STKS[hg % 2]) + STK * (hg // 2 + hg % 2))
                        width = CH if c < i // TPC else (i % TPC + 1) * P
                        pe.matmul(ps[:, 0:width], qs[hg % 2][0:KS, h, P * i:P * (i + 1)],
                                  ks[hg % 2][0:KS, h, CH * c:CH * c + width],
                                  start=True, stop=True).then_inc(s_p2, 1)
                    elif kind == "turned max":
                        pe.wait_ge(s_nm1, b * OUTS + NQ * item[0] + item[1] + 1)
                        pe.transpose(ps.bitcast(BF16)[0:HG * MAXROWS * TPC, 0:P],
                                     nmaxb[:, :, :, :].rearrange("p h r t -> p (h r t)"),
                                     identb[:, :]).then_inc(s_p2, 1)
                    elif kind == "turned out":
                        oq = NQ * item[0] + item[1]
                        pe.wait_ge(s_o1, b * OUTS + oq + 1)
                        for i in range(TPC):
                            ins = pe.transpose(ps[:, P * i:P * (i + 1)], osb[:, oq % 2, P * i:P * (i + 1)],
                                               ident[:, :])
                        ins.then_inc(s_p2, 1)
                    elif kind == "project":
                        t = item[1]
                        if t >= 4:
                            pe.wait_ge(s_ve, b * NT + t - 3)
                        for c in range(DC):
                            ins = pe.matmul(bank(t % 4, 0, D), tok(c, t), wv1[:, c, :],
                                            start=(c == 0), stop=(c == DC - 1))
                        ins.then_inc(s_vp, 1)
                    elif kind == "scores":
                        hg, s = item
                        k, pair = divmod(s, 2)
                        q, kb = ORDER[k]
                        if item == (0, 0):
                            pe.wait_ge(s_ve, b * NT + NT)
                        off = span(q, kb)
                        at = SUBS * hg + s
                        oq = NQ * hg + q
                        if kb == 0 and pair == 0:
                            pe.wait_ge(s_row1[oq % 2], b * (ROWS * OUTS // 2) + ROWS * (oq // 2 + 1))
                        if at >= 2:
                            pe.wait_ge(s_e1, b * NHG * SUBS + at - 1)
                        diagonal = kb >= TPC * q
                        rows = slice(0, KS + MAXROWS)
                        for h in range(2 * pair, 2 * pair + 2):
                            ins = pe.matmul(bank(h, 0, CH - off), ks[hg % 2][rows, h, P * kb:P * (kb + 1)],
                                            qs[hg % 2][rows, h, CH * q + off:CH * (q + 1)],
                                            start=True, stop=not diagonal)
                            if diagonal:
                                ins = pe.matmul(bank(h, 0, P), identb[:, :], maskk[:, :], start=False, stop=True)
                        ins.then_inc(s_s1, 1)
                    elif kind == "values":
                        hg, k = item
                        q, kb = ORDER[k]
                        off = span(q, kb)
                        oq = NQ * hg + q
                        if kb == 0 and oq >= 1:
                            pe.wait_ge(s_o1, b * OUTS + oq)
                        pe.wait_ge(s_e1, b * NHG * SUBS + SUBS * hg + 2 * k + 2)
                        for h in range(HG):
                            ins = pe.matmul(bank(7, off, CH, rows=VW, row=32 * h),
                                            v1[:, kb, HG * hg + h, :], probs[:, HG * (k % 2) + h, 0:CH - off],
                                            start=(kb == 0), stop=last_block(k))
                        ins.then_inc(s_v1, 1)
                turn("AT1", att, lambda g: pe.wait_ge(s_m2, b * UNITS1 + UNITS1))
                by_tiles("WO1", tok, lambda c: wo1[:, c, :], lambda g: turned("AT1", g))

                turn("T3", xn, lambda g: normalised(pe, b, 3, g))
                pe.wait_ge(s_w1, W1)
                by_tiles("R", lambda c, t: xr[:, c, P * t:P * (t + 1)], lambda c: wr[:, c, :],
                         lambda g: pe.wait_ge(s_mix, b * NQ + g + 1))
                for n in range(2 * NQ):
                    q, half = divmod(n, DC)
                    ps = job("K", n)
                    for c in range(DC):
                        last = pe.matmul(ps, wk[:, c, P * half:P * (half + 1)], xk[:, c, CH * q:CH * (q + 1)],
                                         start=(c == 0), stop=(c == DC - 1))
                    last.then_inc(s_mm, 1)
                by_tiles("V", lambda c, t: kact[:, c, P * t:P * (t + 1)], lambda c: wv[:, c, :],
                         lambda g: pe.wait_ge(s_ku, b * 8 + 2 * (g + 1)))


def rope_tables():
    theta = (np.float32(1.0) / np.float32(10000.0) ** (np.arange(0, DK1, 2, dtype=np.float32) / np.float32(DK1)))
    angle = np.outer(np.arange(T, dtype=np.float32), theta.astype(np.float32)).astype(np.float32)
    angle = np.concatenate([angle, angle], axis=-1)
    sign = np.where(np.arange(DK1) < DK1 // 2, np.float32(-1), np.float32(1))
    return np.cos(angle).astype(np.float32), (np.sin(angle) * sign).astype(np.float32)


def arrays(inputs):
    a = {k.replace("L0_attn_", "a0_").replace("L0_ffn_", "f0_").replace("L1_attn_", "a1_").replace("L1_ffn_", "f1_"):
         np.asarray(v) for k, v in inputs.items()}
    c, s = rope_tables()
    w = {
        "wqk0": np.concatenate([a["a0_Wq"], a["a0_Wk"]]).T, "wv0": a["a0_Wv"].T, "wo0": a["a0_Wo"].T,
        "bqk0": np.stack([a["a0_bq"], a["a0_bk"]]).T, "bv0": a["a0_bv"], "bo0": a["a0_bo"],
        "wf": a["f0_weight"].T, "bf": a["f0_bias"],
        "wqk1": np.concatenate([a["a1_W_Q"], a["a1_W_K"]]).T, "wv1": a["a1_W_V"].T, "wo1": a["a1_W_O"].T,
        "wr": a["f1_W_r"].T, "wk": a["f1_W_k"].T, "wv": a["f1_W_v"].T,
        "mu": np.stack([a["f1_mu_r"], a["f1_mu_k"]]).reshape(2, DC, P).transpose(2, 0, 1), "cos": c, "sin": s,
    }
    return a["a0_y_all"], {k: np.ascontiguousarray(v) for k, v in w.items()}


def kernel(**inputs):
    import concourse.bacc as bacc
    from concourse.bass_utils import run_bass_kernel_spmd

    nc = bacc.Bacc("TRN2", target_bir_lowering=False, num_devices=1)
    x, w = arrays(inputs)
    x_in = nc.dram_tensor("x_in", x.shape, F32, kind="ExternalInput").ap()
    aps = {k: nc.dram_tensor("w_" + k, v.shape, F32, kind="ExternalInput").ap() for k, v in w.items()}
    y = nc.dram_tensor("y_out", (B, T, D), F32, kind="ExternalOutput").ap()
    build(nc, x_in, y, aps)
    r = run_bass_kernel_spmd(nc, [{"x_in": x, **{"w_" + k: v for k, v in w.items()}}], core_ids=[0])
    return r.results[0]["y_out"]
```
